# Optimizing a Trainium2 kernel written in Bass

```python
import numpy as np
import jax
import jax.numpy as jnp

def _softmax(x, axis=-1):
    return jax.nn.softmax(x, axis=axis)

def _gelu(x):
    return jax.nn.gelu(x, approximate=True)

def _silu(x):
    return jax.nn.silu(x)

def _sigmoid(x):
    return jax.nn.sigmoid(x)

def _layernorm(x, axis=-1, eps=1e-05):
    m = jnp.mean(x, axis=axis, keepdims=True)
    v = jnp.var(x, axis=axis, keepdims=True)
    return (x - m) / jnp.sqrt(v + eps)

def _scatter_add(tgt, idx, src, axis=0):
    return tgt.at[idx].add(src)

def _segment_sum(src, seg, n):
    return jax.ops.segment_sum(src, seg, n)
kernel_name = 'mk_adj_preln_d1_adj_r2_12b02e'

def setup_inputs(seed: int=0):
    np.random.seed(seed)
    _w = jnp.asarray

    def _rec_inputs():
        import jax
        import jax.numpy as jnp
        _gk = jax.random.key(seed)
        x = 7.22e-05 + 1 * jax.random.normal(jax.random.fold_in(_gk, 1), (8, 1024, 256), jnp.float32)
        _w = (1.0 + jnp.arange(1024, dtype=jnp.float32)) ** (-0.5)
        _w = _w / _w.mean()
        _pij = jnp.clip(0.00390625 * _w[:, None] * _w[None, :], 0.0, 1.0)
        _a = jax.random.uniform(jax.random.fold_in(_gk, 2), (8, 1024, 1024)) < _pij
        _a = jnp.logical_or(_a, jnp.swapaxes(_a, -1, -2))
        _a = jnp.logical_or(_a, jnp.eye(1024, dtype=bool))
        _af = _a.astype(jnp.float32)
        _af = _af * jax.random.uniform(jax.random.fold_in(_gk, 3), (8, 1024, 1024), jnp.float32, 0.05, 1)
        adj = _af
        return (x, adj)
    x, adj = _rec_inputs()

    def _L0_gnn_setup():
        import jax, jax.numpy as jnp
        import numpy as np
        EPS_LN = 1e-05

        def hypergraph_conv(x, adj, W, b):
            N, C, _ = adj.shape
            H = (adj != 0).astype(x.dtype)
            w = adj.reshape(N, -1)[:, :C]
            xw = jnp.einsum('ncd,hd->nch', x, W)
            Dn = jnp.einsum('nce,ne->nc', H, w)
            Dn = jnp.where(Dn > 0, 1.0 / Dn, 0.0)
            Be = H.sum(axis=1)
            Be = jnp.where(Be > 0, 1.0 / Be, 0.0)
            m = Be[:, :, None] * jnp.einsum('nce,nch->neh', H, xw)
            out = Dn[:, :, None] * jnp.einsum('nce,neh->nch', H, m)
            return out + b

        def layer_norm(x, g, b):
            mu = jnp.mean(x, axis=-1, keepdims=True)
            var = jnp.var(x, axis=-1, keepdims=True)
            return (x - mu) * jax.lax.rsqrt(var + EPS_LN) * g + b
        key = jax.random.key(seed)
        ks = jax.random.split(key, 4)
        N, C, Din, Dh, Dout = (16, 512, 256, 512, 256)
        x = jax.random.normal(ks[0], (N, C, Din), dtype=jnp.float32)
        adj = jax.random.uniform(ks[1], (N, C, C), dtype=jnp.float32, minval=0.1, maxval=1.0)
        W1 = jax.random.normal(ks[2], (Dh, Din), dtype=jnp.float32) * (1.0 / np.sqrt(Din))
        b1 = jnp.zeros((Dh,), dtype=jnp.float32)
        gamma = jnp.ones((Dh,), dtype=jnp.float32)
        beta = jnp.zeros((Dh,), dtype=jnp.float32)
        W2 = jax.random.normal(ks[3], (Dout, Dh), dtype=jnp.float32) * (1.0 / np.sqrt(Dh))
        b2 = jnp.zeros((Dout,), dtype=jnp.float32)
        return {'x': x, 'adj': adj, 'W1': W1, 'b1': b1, 'gamma': gamma, 'beta': beta, 'W2': W2, 'b2': b2}
    _L0_gnn_all = _L0_gnn_setup()
    _L0_gnn_in = {k: v for k, v in _L0_gnn_all.items() if k in ('W1', 'b1', 'gamma', 'beta', 'W2', 'b2')}
    del _L0_gnn_all
    return {'x': x, 'adj': adj, 'L0_gnn_W1': _L0_gnn_in['W1'], 'L0_gnn_b1': _L0_gnn_in['b1'], 'L0_gnn_gamma': _L0_gnn_in['gamma'], 'L0_gnn_beta': _L0_gnn_in['beta'], 'L0_gnn_W2': _L0_gnn_in['W2'], 'L0_gnn_b2': _L0_gnn_in['b2']}

def reference(x, adj, L0_gnn_W1, L0_gnn_b1, L0_gnn_gamma, L0_gnn_beta, L0_gnn_W2, L0_gnn_b2):
    import jax
    import jax.numpy as jnp

    def _L0_gnn_ref(x, adj, W1, b1, gamma, beta, W2, b2):
        import jax, jax.numpy as jnp
        import numpy as np
        EPS_LN = 1e-05

        def hypergraph_conv(x, adj, W, b):
            N, C, _ = adj.shape
            H = (adj != 0).astype(x.dtype)
            w = adj.reshape(N, -1)[:, :C]
            xw = jnp.einsum('ncd,hd->nch', x, W)
            Dn = jnp.einsum('nce,ne->nc', H, w)
            Dn = jnp.where(Dn > 0, 1.0 / Dn, 0.0)
            Be = H.sum(axis=1)
            Be = jnp.where(Be > 0, 1.0 / Be, 0.0)
            m = Be[:, :, None] * jnp.einsum('nce,nch->neh', H, xw)
            out = Dn[:, :, None] * jnp.einsum('nce,neh->nch', H, m)
            return out + b

        def layer_norm(x, g, b):
            mu = jnp.mean(x, axis=-1, keepdims=True)
            var = jnp.var(x, axis=-1, keepdims=True)
            return (x - mu) * jax.lax.rsqrt(var + EPS_LN) * g + b
        h = jax.nn.relu(hypergraph_conv(x, adj, W1, b1))
        h = layer_norm(h, gamma, beta)
        y = hypergraph_conv(h, adj, W2, b2)
        return y + x
    h = jnp.maximum(_layernorm(x, axis=-1), 0.0)
    x = x + _L0_gnn_ref(h, adj, L0_gnn_W1, L0_gnn_b1, L0_gnn_gamma, L0_gnn_beta, L0_gnn_W2, L0_gnn_b2)
    return x

_drawn_inputs = setup_inputs


def setup_inputs(seed=0):
    import zlib

    import numpy as np

    out = dict(_drawn_inputs(seed))
    spreads = {'L0_gnn_b1': (0.0, 0.1),
     'L0_gnn_gamma': (1.0, 0.2),
     'L0_gnn_beta': (0.0, 0.1),
     'L0_gnn_b2': (0.0, 0.8)}
    factors = {}
    for name, (base, spread) in spreads.items():
        noise = np.random.default_rng([zlib.crc32(name.encode()), seed]).standard_normal(out[name].shape)
        drawn = base * np.exp(spread * noise) if base else spread * noise
        out[name] = jnp.asarray(drawn.astype(out[name].dtype))
    for name, factor in factors.items():
        out[name] = (out[name] * factor).astype(out[name].dtype)
    return out
```

```python
from contextlib import ExitStack

import concourse.bass as bass
from concourse import mybir

ALU = mybir.AluOpType
ACT = mybir.ActivationFunctionType
RMAX = bass.bass_isa.ReduceOp.max
F32 = mybir.dt.float32
F16 = mybir.dt.float16
BF16 = mybir.dt.bfloat16
U32 = mybir.dt.uint32

P = 128
BANK = 512
HI, LO = 0, 1

H0_SCALE = 2.0 ** 8
PT_SCALE = 2.0 ** -7
W_SCALE = 2.0 ** 8
ZN_SCALE = 2.0 ** 4
XW_SCALE = 2.0 ** -7
BIAS_ROOM = 2.0 ** -8
TINY = 2.0 ** -100
LEAST = 2.0 ** -126
EXPONENT = 0x7F800000
EPS = 1e-5


class Batch:

    def __init__(self, loop, offset):
        self.loop, self.offset, self.slot = loop, offset, offset % 2

    def next(self, k):
        return Batch(self.loop, self.offset + k)

    def index(self):
        return self.loop + self.offset

    def count(self, per_batch, more):
        return self.loop * per_batch + (self.offset * per_batch + more)


def wait_reuse(eng, sem, value):
    if not (isinstance(value, int) and value <= 0):
        eng.wait_ge(sem, value)


def hypergraph_block(nc, x, adj, w1t, b1, gamma, beta, w2t, b2, out):
    N, C, DIN = x.shape
    DH = w1t.shape[1]
    DOUT = w2t.shape[1]
    T = C // P
    DT = DIN // P
    HT_ = DH // P
    assert C == 1024 and T == 8 and DIN == DOUT == 256 and DH == BANK and N % 2 == 0 and N >= 4
    ONE = DIN
    LO_AT = DIN + 8
    HL = LO_AT + DIN
    GROUPS = 4
    GT = T // GROUPS
    QUARTERS = 4
    QT = T // QUARTERS
    X_STEPS, Z_STEPS, N_STEPS = 10, 10, 5
    ZRING = 4

    with ExitStack() as ctx:
        def sb(name, shape, dt=F32):
            return ctx.enter_context(nc.sbuf_tensor(name, shape, dt))

        def sem(name):
            return ctx.enter_context(nc.semaphore(name))

        adj_in = sb("adj_in", [P, T, C])
        inc = sb("incidence", [P, 2, T, C], BF16)
        inc_t = sb("incidence_t", [P, 2, T, C], BF16)
        x_in = sb("x_in", [P, T, DIN])
        u = sb("h0_ring", [P, 2, GT, DIN])
        h0 = sb("h0_split", [P, T, HL], F16)
        res = sb("residual", [P, 2, T, DOUT])
        edge = sb("edge_means", [P, T, 2, DIN], F16)
        pt = sb("pt_split", [P, DT, 2, C], F16)
        z = sb("z", [P, T, DH])
        zt = sb("zt_ring", [P, ZRING, 2, DH], F16)
        xw = sb("xw_split", [P, T, 2, DOUT], F16)
        xf = sb("xw_ring", [P, 2, DOUT])
        w1s = sb("w1_split", [P, DT, 2, DH], F16)
        w2s = sb("w2_split", [P, HT_, 2, DOUT], F16)
        b1_row = sb("b1_row", [P, DH])
        b2_row = sb("b2_row", [P, DOUT])
        bw_row = sb("bias_w2_row", [P, DOUT])
        edge_w = sb("edge_weights", [P, C])
        junk = sb("junk", [P, C])
        ident32 = sb("ident32", [P, P])
        stat = sb("stat", [P, T, 6])
        x_ln = sb("x_ln", [P, 6, T])
        z_ln = sb("z_ln", [P, 6, T])
        deg = sb("node_degree", [P, T])
        dn_tmp = sb("dn_tmp", [P, 3, T])
        dn1 = sb("dn_conv1", [P, 2, T])
        dn2 = sb("dn_conv2", [P, 2, T])
        be_cnt = sb("edge_count", [P, T])
        be = sb("edge_inverse", [P, 2, T])
        gb = sb("gamma_beta", [P, 2, HT_])
        wm = sb("weight_max", [P, 4])
        wext = sb("weight_extremes", [P, 3, 2])
        wall = sb("weight_max_all", [P, 2])
        wp = sb("weight_power", [P, 2])
        wr = sb("weight_factor", [P, 6])
        w1f = z[:, 0:2, :]
        w2f = z[:, 2:4, :].rearrange("p a (b o) -> p (a b) o", o=DOUT)
        gf = z[:, 4:6, :].rearrange("p a (b o) -> p (a b) o", o=DOUT)
        beta_cols = z[:, 6, :].rearrange("p (t m) -> p t m", m=P)

        narrow = [ctx.enter_context(nc.psum_tensor(f"narrow{i}", [P, BANK], F32)) for i in range(4)]
        wide = [ctx.enter_context(nc.psum_tensor(f"wide{i}", [P, BANK], F32)) for i in range(4)]

        x_loaded = sem("x_loaded")
        w_loaded = sem("w_loaded")
        adj_loaded = [sem(f"adj_loaded{q}") for q in range(QUARTERS)]
        weights_loaded = sem("weights_loaded")
        rows_loaded = sem("rows_loaded")
        stored = [sem(f"stored{h}") for h in range(2)]
        consts_set = sem("consts_set")
        max_here = sem("max_here")
        max_all = sem("max_all")
        setup_step = sem("setup_step")
        max_step = sem("max_step")
        beta_ready = sem("beta_ready")
        bias_done = sem("bias_done")
        w_hi = sem("w_hi")
        w_ready = sem("w_ready")
        x_stat = sem("x_stat")
        x_step = sem("x_step")
        u_ready = sem("u_ready")
        u_relu = sem("u_relu")
        h0_ready = sem("h0_ready")
        x_added = sem("x_added")
        res_ready = sem("res_ready")
        inc_ready = sem("inc_ready")
        deg_done = sem("deg_done")
        dn_step = sem("dn_step")
        a_done = sem("a_done")
        be_step = sem("be_step")
        t1_hi = sem("t1_hi")
        t1_ready = sem("t1_ready")
        inc_t_ready = sem("inc_t_ready")
        b_done = sem("b_done")
        pt_hi = sem("pt_hi")
        pt_ready = sem("pt_ready")
        c_done = sem("c_done")
        c_drained = sem("c_drained")
        z_relu = sem("z_relu")
        z_stat = sem("z_stat")
        z_step = sem("z_step")
        zn_ready = sem("zn_ready")
        zt_done = sem("zt_done")
        zt_hi = sem("zt_hi")
        zt_ready = sem("zt_ready")
        d_done = sem("d_done")
        xf_ready = sem("xf_ready")
        xw_hi = sem("xw_hi")
        xw_ready = sem("xw_ready")
        e_done = sem("e_done")
        t2_hi = sem("t2_hi")
        t2_ready = sem("t2_ready")
        f_done = sem("f_done")
        out_ready = sem("out_ready")

        def rows(ap, b):
            if isinstance(b.loop, int):
                part = ap[b.offset:b.offset + 1]
            else:
                part = ap[bass.ds(b.index(), 1)]
            return part.rearrange("b (p t) d -> p (b t) d", t=T)

        block = ctx.enter_context(nc.Block())

        @block.sync
        def _(sp):
            def load_x(b):
                wait_reuse(sp, res_ready, b.count(1, 0))
                sp.dma_start(x_in[:, :, :], rows(x, b)).then_inc(x_loaded, 16)

            def load_adj(b):
                for q in range(QUARTERS):
                    wait_reuse(sp, inc_ready, b.count(T, QT * (q + 1) - T))
                    wait_reuse(sp, deg_done, b.count(T, QT * (q + 1) - T))
                    sp.dma_start(adj_in[:, QT * q:QT * (q + 1), :],
                                 rows(adj, b)[:, QT * q:QT * (q + 1), :]).then_inc(adj_loaded[q], 16)

            def load_edge_weights(b):
                wait_reuse(sp, f_done, b.count(T, -2 * T))
                wait_reuse(sp, deg_done, b.count(T, 0))
                if isinstance(b.loop, int):
                    first = adj[b.offset:b.offset + 1, 0, :]
                else:
                    first = adj[bass.ds(b.index(), 1), 0, :]
                sp.dma_start(edge_w[:, :], first.to_broadcast([P, C])).then_inc(w_loaded, 16)

            def transpose_inc(b):
                for ct in range(T):
                    sp.dma_start_transpose(inc_t[:, b.slot, :, P * ct:P * (ct + 1)],
                                           inc[:, b.slot, ct, :]).then_inc(inc_t_ready, 16)

            def step(b):
                load_adj(b.next(1))
                load_edge_weights(b.next(1))
                transpose_inc(b)
                load_x(b.next(1))

            load_x(Batch(0, 0))
            sp.dma_start(w1f, w1t.rearrange("(t p) h -> p t h", p=P)).then_inc(weights_loaded, 16)
            sp.dma_start(w2f, w2t.rearrange("(t p) o -> p t o", p=P)).then_inc(weights_loaded, 16)
            sp.dma_start(gb[:, 0, :], gamma).then_inc(weights_loaded, 16)
            sp.dma_start(gb[:, 1, :], beta).then_inc(weights_loaded, 16)
            load_edge_weights(Batch(0, 0))
            load_adj(Batch(0, 0))
            sp.dma_start(b2_row[:, :], b2.to_broadcast([P, DOUT])).then_inc(rows_loaded, 16)
            sp.dma_start(b1_row[:, :], b1.to_broadcast([P, DH])).then_inc(rows_loaded, 16)
            for k in range(3):
                step(Batch(0, k))
            with sp.Fori(2, N - 3, 2) as n:
                for k in range(2):
                    step(Batch(n, k + 1))
            sp.wait_ge(f_done, T * (N - 2))
            sp.wait_ge(inc_ready, T * N)
            transpose_inc(Batch(0, N - 1))

        @block.gpsimd
        def _(pool):
            nc.gpsimd.memset(ident32[:, :], 0.0).then_inc(consts_set, 1)
            nc.gpsimd.memset(h0[:, :, ONE:ONE + 1], 1.0).then_inc(consts_set, 1)
            pool.wait_ge(consts_set, 2)
            nc.gpsimd.affine_select(out=ident32[:, :], in_=ident32[:, :], compare_op=ALU.not_equal, fill=1.0, base=0,
                                    pattern=[[-1, P]], channel_multiplier=1).then_inc(consts_set, 1)
            pool.wait_ge(max_here, 1)
            nc.gpsimd.partition_all_reduce(wall[:, :], wm[:, 0:2], P, RMAX).then_inc(max_all, 1)
            pool.wait_ge(rows_loaded, 32)

            def add_h0(b):
                for g in range(GROUPS):
                    pool.wait_ge(u_relu, b.count(GROUPS, g + 1))
                    xs = x_in[:, GT * g:GT * (g + 1), :]
                    nc.gpsimd.tensor_tensor(xs, xs, u[:, g % 2, :, :], ALU.add).then_inc(x_added, 1)

            def residual(b):
                pool.wait_ge(x_added, b.count(GROUPS, GROUPS))
                for h in range(2):
                    wait_reuse(pool, stored[h], b.count(16, -16))
                nc.gpsimd.tensor_tensor(res[:, b.slot, :, :], x_in[:, :, :],
                                        b2_row[:, None, :].to_broadcast([P, T, DOUT]),
                                        ALU.add).then_inc(res_ready, 1)

            def store(b):
                for h in range(2):
                    pool.wait_ge(out_ready, b.count(T, T // 2 * (h + 1)))
                    part = slice(T // 2 * h, T // 2 * (h + 1))
                    pool.dma_start(rows(out, b)[:, part, :], res[:, b.slot, part, :]).then_inc(stored[h], 16)

            for k in range(2):
                add_h0(Batch(0, k))
                residual(Batch(0, k))
            with pool.Fori(0, N - 2, 2) as n:
                for k in range(2):
                    add_h0(Batch(n, k + 2))
                    store(Batch(n, k))
                    residual(Batch(n, k + 2))
            store(Batch(0, N - 2))
            store(Batch(0, N - 1))
            for h in range(2):
                pool.wait_ge(stored[h], 16 * N)

        @block.tensor
        def _(pe):
            def take_narrow(b, t, own, before, b_before):
                if t >= 4:
                    pe.wait_ge(own, b.count(T, t - 3))
                elif b_before is not None:
                    pe.wait_ge(before, b_before.count(T, t + 5))
                return narrow[t % 4]

            def stage_a(b):
                opening = isinstance(b.loop, int) and b.offset < 2
                pe.wait_ge(inc_ready, b.count(T, T))
                pe.wait_ge(h0_ready, b.count(GROUPS, GROUPS))
                if isinstance(b.loop, int) and b.offset == 0:
                    pe.wait_ge(consts_set, 3)
                for et in range(T):
                    if opening:
                        acc = take_narrow(b, et, t1_ready, t1_ready, b.next(-1) if b.offset else None)
                    else:
                        acc = take_narrow(b, et, t1_ready, out_ready, b.next(-2))
                    cols = slice(P * et, P * (et + 1))
                    for ct in range(T):
                        nc.tensor.matmul(acc[:, 0:ONE + 1], inc[:, b.slot, ct, cols], h0[:, ct, 0:ONE + 1],
                                         start=(ct == 0), stop=False)
                        last = nc.tensor.matmul(acc[:, 0:DIN], inc[:, b.slot, ct, cols], h0[:, ct, LO_AT:HL],
                                                start=False, stop=(ct == T - 1))
                    last.then_inc(a_done, 1)

            def stage_b(b):
                pe.wait_ge(inc_t_ready, b.count(16 * T, 16 * T))
                for j in range(4):
                    dt, half = j % 2, j // 2
                    wait_reuse(pe, zt_ready, b.count(T, 5 + j - T))
                    for et in range(T):
                        if j == 0:
                            pe.wait_ge(t1_ready, b.count(T, et + 1))
                        for part in (HI, LO):
                            last = nc.tensor.matmul(wide[j][:, :], edge[:, et, part, P * dt:P * (dt + 1)],
                                                    inc_t[:, b.slot, et, BANK * half:BANK * (half + 1)],
                                                    start=(et == 0 and part == HI), stop=(et == T - 1 and part == LO))
                    last.then_inc(b_done, 1)

            def stage_c(b):
                if isinstance(b.loop, int) and b.offset == 0:
                    pe.wait_ge(w_ready, 2)
                for t in range(T):
                    pe.wait_ge(pt_ready, b.count(4, max(2 * (t // 4 + 1), min(t + 1, 4))))
                    if t >= 4:
                        pe.wait_ge(c_drained, b.count(T, t - 3))
                    k = 0
                    for dt in range(DT):
                        for left, right in ((HI, HI), (HI, LO), (LO, HI)):
                            last = nc.tensor.matmul(wide[t % 4][:, :], pt[:, dt, left, P * t:P * (t + 1)],
                                                    w1s[:, dt, right, :], start=(k == 0), stop=(k == 3 * DT - 1))
                            k += 1
                    last.then_inc(c_done, 1)

            def stage_d(b):
                final = isinstance(b.loop, int) and b.offset == N - 1

                def turn(t):
                    pe.wait_ge(zn_ready, b.count(T, t + 1))
                    if t < 4:
                        pe.wait_ge(c_drained, b.count(T, 5 + t))
                    else:
                        pe.wait_ge(zt_ready, b.count(T, t - 3))
                    for ht in range(HT_):
                        last = nc.tensor.transpose(wide[t % 4][:, P * ht:P * (ht + 1)], z[:, t, P * ht:P * (ht + 1)],
                                                   ident32[:, :])
                    last.then_inc(zt_done, 1)

                for t in range(3):
                    turn(t)
                for t in range(T):
                    if final:
                        acc = take_narrow(b, t, xf_ready, out_ready, b.next(-1))
                    else:
                        acc = take_narrow(b, t, xf_ready, t1_ready, b.next(1))
                    pe.wait_ge(zt_ready, b.count(T, t + 1))
                    k = 0
                    for ht in range(HT_):
                        for left, right in ((HI, HI), (HI, LO), (LO, HI)):
                            last = nc.tensor.matmul(acc[:, 0:DOUT], zt[:, t % ZRING, left, P * ht:P * (ht + 1)],
                                                    w2s[:, ht, right, :], start=(k == 0), stop=(k == 3 * HT_ - 1))
                            k += 1
                    last.then_inc(d_done, 1)
                    if t + 3 < T:
                        turn(t + 3)

            def stage_e(b):
                for et in range(T):
                    acc = take_narrow(b, et, t2_ready, xf_ready, b)
                    for ct in range(T):
                        if et == 0:
                            pe.wait_ge(xw_ready, b.count(T, ct + 1))
                        for part in (HI, LO):
                            last = nc.tensor.matmul(acc[:, 0:DOUT], inc[:, b.slot, ct, P * et:P * (et + 1)],
                                                    xw[:, ct, part, :],
                                                    start=(ct == 0 and part == HI), stop=(ct == T - 1 and part == LO))
                    last.then_inc(e_done, 1)

            def stage_f(b):
                for ct in range(T):
                    acc = take_narrow(b, ct, out_ready, t2_ready, b)
                    for et in range(T):
                        if ct == 0:
                            pe.wait_ge(t2_ready, b.count(T, et + 1))
                        for part in (HI, LO):
                            last = nc.tensor.matmul(acc[:, 0:DOUT], inc_t[:, b.slot, et, P * ct:P * (ct + 1)],
                                                    edge[:, et, part, :],
                                                    start=(et == 0 and part == HI), stop=(et == T - 1 and part == LO))
                    last.then_inc(f_done, 1)

            pe.wait_ge(weights_loaded, 64)
            pe.wait_ge(beta_ready, 1)
            for ht in range(HT_):
                last = nc.tensor.matmul(wide[3][:, 0:DOUT], beta_cols[:, ht, :], w2f[:, ht, :],
                                        start=(ht == 0), stop=(ht == HT_ - 1))
            last.then_inc(bias_done, 1)

            stage_a(Batch(0, 0))
            stage_b(Batch(0, 0))
            stage_c(Batch(0, 0))
            stage_a(Batch(0, 1))
            with pe.Fori(0, N - 2, 2) as n:
                for k in range(2):
                    stage_d(Batch(n, k))
                    stage_b(Batch(n, k + 1))
                    stage_e(Batch(n, k))
                    stage_c(Batch(n, k + 1))
                    stage_f(Batch(n, k))
                    stage_a(Batch(n, k + 2))
            stage_d(Batch(0, N - 2))
            stage_b(Batch(0, N - 1))
            stage_e(Batch(0, N - 2))
            stage_c(Batch(0, N - 1))
            stage_f(Batch(0, N - 2))
            stage_d(Batch(0, N - 1))
            stage_e(Batch(0, N - 1))
            stage_f(Batch(0, N - 1))

        @block.scalar
        def _(act):
            def copy(o, i, **kw):
                return nc.scalar.activation(o, i, ACT.Copy, **kw)

            def root_x(b):
                act.wait_ge(x_step, b.count(X_STEPS, 4))
                nc.scalar.activation(x_ln[:, 1, :], x_ln[:, 0, :], ACT.Sqrt).then_inc(x_step, 1)

            def relu_x(b, g):
                act.wait_ge(u_ready, b.count(T, GT * (g + 1)))
                if g == 0:
                    wait_reuse(act, a_done, b.count(T, 0))
                ug = u[:, g % 2, :, :]
                nc.scalar.activation(h0[:, GT * g:GT * (g + 1), 0:DIN], ug, ACT.Relu, scale=H0_SCALE)
                nc.scalar.activation(ug, ug, ACT.Relu).then_inc(u_relu, 1)

            def drain_b(b, j):
                act.wait_ge(b_done, b.count(4, j + 1))
                if j == 0:
                    wait_reuse(act, c_done, b.count(T, 0))
                dt, half = j % 2, j // 2
                copy(pt[:, dt, HI, BANK * half:BANK * (half + 1)], wide[j][:, :], scale=PT_SCALE).then_inc(pt_hi, 1)

            def phase_b(b, bx):
                drain_b(b, 0)
                if bx is not None:
                    root_x(bx)
                    relu_x(bx, 0)
                drain_b(b, 1)
                if bx is not None:
                    relu_x(bx, 1)
                    relu_x(bx, 2)
                drain_b(b, 2)
                if bx is not None:
                    relu_x(bx, 3)
                drain_b(b, 3)

            def phase_c(b):
                for t in range(T):
                    act.wait_ge(c_drained, b.count(T, t + 1))
                    nc.scalar.activation(z[:, t, :], z[:, t, :], ACT.Relu).then_inc(z_relu, 1)
                act.wait_ge(z_step, b.count(Z_STEPS, 4))
                nc.scalar.activation(z_ln[:, 1, :], z_ln[:, 0, :], ACT.Sqrt).then_inc(z_step, 1)

            def phase_d(b):
                def turn_hi(t):
                    act.wait_ge(zt_done, b.count(T, t + 1))
                    if t >= ZRING:
                        act.wait_ge(d_done, b.count(T, t + 1 - ZRING))
                    copy(zt[:, t % ZRING, HI, :], wide[t % 4][:, :]).then_inc(zt_hi, 1)

                for t in range(3):
                    turn_hi(t)
                for t in range(T):
                    act.wait_ge(xf_ready, b.count(T, t + 1))
                    copy(xw[:, t, HI, :], xf[:, t % 2, :]).then_inc(xw_hi, 1)
                    if t + 3 < T:
                        turn_hi(t + 3)

            def phase_e(b):
                if isinstance(b.loop, int) and b.offset == N - 1:
                    act.wait_ge(f_done, b.count(T, 0))
                else:
                    act.wait_ge(b_done, b.count(4, 8))
                for et in range(T):
                    act.wait_ge(e_done, b.count(T, et + 1))
                    copy(edge[:, et, HI, :], narrow[et % 4][:, 0:DOUT], scale=be[:, b.slot, et:et + 1]).then_inc(t2_hi, 1)

            def phase_a(b):
                wait_reuse(act, f_done, b.count(T, -T))
                if isinstance(b.loop, int) and b.offset == 1:
                    act.wait_ge(b_done, 4)
                for et in range(T):
                    act.wait_ge(be_step, b.count(2 * T, 2 * et + 2))
                    copy(edge[:, et, HI, :], narrow[et % 4][:, 0:DIN], scale=be[:, b.slot, et:et + 1]).then_inc(t1_hi, 1)

            root_x(Batch(0, 0))
            for g in range(GROUPS):
                relu_x(Batch(0, 0), g)
            act.wait_ge(setup_step, 6)
            copy(w1s[:, :, HI, :], w1f).then_inc(w_hi, 1)
            act.wait_ge(setup_step, 7)
            copy(w2s[:, :, HI, :], gf).then_inc(w_hi, 1)
            phase_a(Batch(0, 0))
            phase_b(Batch(0, 0), Batch(0, 1))
            phase_c(Batch(0, 0))
            phase_a(Batch(0, 1))
            with act.Fori(0, N - 2, 2) as n:
                for k in range(2):
                    phase_d(Batch(n, k))
                    phase_b(Batch(n, k + 1), Batch(n, k + 2))
                    phase_e(Batch(n, k))
                    phase_c(Batch(n, k + 1))
                    phase_a(Batch(n, k + 2))
            phase_d(Batch(0, N - 2))
            phase_b(Batch(0, N - 1), None)
            phase_e(Batch(0, N - 2))
            phase_c(Batch(0, N - 1))
            phase_d(Batch(0, N - 1))
            phase_e(Batch(0, N - 1))

        @block.vector
        def _(dve):
            V = nc.vector

            def variance(ln, stat_sem, step_sem, b, steps, n):
                s, _, y, tmp, _, mean = (ln[:, i, :] for i in range(6))
                dve.wait_ge(stat_sem, b.count(T, T))
                V.tensor_tensor(mean, stat[:, :, 1], stat[:, :, 4], ALU.add)
                V.tensor_tensor(tmp, stat[:, :, 1], stat[:, :, 4], ALU.subtract)
                V.tensor_tensor(s, stat[:, :, 2], stat[:, :, 5], ALU.add).then_inc(step_sem, 1)
                dve.wait_ge(step_sem, b.count(steps, 1))
                V.tensor_scalar(mean, mean, 0.5, None, ALU.mult)
                V.tensor_tensor(y, tmp, tmp, ALU.mult).then_inc(step_sem, 1)
                dve.wait_ge(step_sem, b.count(steps, 2))
                V.scalar_tensor_tensor(out=tmp, in0=s, scalar=4.0 / n, in1=y, op0=ALU.mult,
                                       op1=ALU.add).then_inc(step_sem, 1)
                dve.wait_ge(step_sem, b.count(steps, 3))
                V.tensor_scalar(s, tmp, 0.25, EPS, ALU.mult, ALU.add).then_inc(step_sem, 1)

            def inverse_root(ln, step_sem, b, steps, scale):
                s, root, y, tmp, rstd = (ln[:, i, :] for i in range(5))
                dve.wait_ge(step_sem, b.count(steps, 5))
                V.reciprocal(y, root).then_inc(step_sem, 1)
                dve.wait_ge(step_sem, b.count(steps, 6))
                V.tensor_tensor(tmp, y, y, ALU.mult).then_inc(step_sem, 1)
                dve.wait_ge(step_sem, b.count(steps, 7))
                V.tensor_tensor(tmp, tmp, s, ALU.mult).then_inc(step_sem, 1)
                dve.wait_ge(step_sem, b.count(steps, 8))
                V.tensor_scalar(tmp, tmp, -0.5 * scale, 1.5 * scale, ALU.mult, ALU.add).then_inc(step_sem, 1)
                dve.wait_ge(step_sem, b.count(steps, 9))
                V.tensor_tensor(rstd, tmp, y, ALU.mult).then_inc(step_sem, 1)

            def x_stats(b):
                dve.wait_ge(x_loaded, b.count(16, 16))
                for t in range(T):
                    V.bn_stats(stat[:, t, :], x_in[:, t, :]).then_inc(x_stat, 1)
                variance(x_ln, x_stat, x_step, b, X_STEPS, DIN)

            def x_normalise(b, g):
                if g == 0:
                    dve.wait_ge(x_step, b.count(X_STEPS, X_STEPS))
                wait_reuse(dve, x_added, b.count(GROUPS, g - 1))
                wait_reuse(dve, h0_ready, b.count(GROUPS, g - 1))
                for i in range(GT):
                    t = GT * g + i
                    V.tensor_scalar(u[:, g % 2, i, :], x_in[:, t, :], x_ln[:, 5, t:t + 1], x_ln[:, 4, t:t + 1],
                                    ALU.subtract, ALU.mult).then_inc(u_ready, 1)

            def h0_lo(b, g):
                dve.wait_ge(u_relu, b.count(GROUPS, g + 1))
                ts = slice(GT * g, GT * (g + 1))
                V.scalar_tensor_tensor(out=h0[:, ts, LO_AT:HL], in0=u[:, g % 2, :, :], scalar=H0_SCALE,
                                       in1=h0[:, ts, 0:DIN], op0=ALU.mult, op1=ALU.subtract).then_inc(h0_ready, 1)

            def incidence(b, q):
                dve.wait_ge(adj_loaded[q], b.count(16, 16))
                if q == 0:
                    wait_reuse(dve, e_done, b.count(T, -T))
                for ct in range(QT * q, QT * (q + 1)):
                    V.tensor_scalar(inc[:, b.slot, ct, :], adj_in[:, ct, :], 0.0, None,
                                    ALU.not_equal).then_inc(inc_ready, 1)

            def degree(b, ct):
                if ct == 0:
                    dve.wait_ge(w_loaded, b.count(16, 16))
                if ct % QT == 0:
                    dve.wait_ge(adj_loaded[ct // QT], b.count(16, 16))
                wait_reuse(dve, deg_done, b.count(T, ct))
                V.scalar_tensor_tensor(out=junk[:, :], in0=adj_in[:, ct, :], scalar=0.0, in1=edge_w[:, :],
                                       op0=ALU.not_equal, op1=ALU.mult,
                                       accum_out=deg[:, ct:ct + 1]).then_inc(deg_done, 1)

            def node_inverse(b):
                dve.wait_ge(deg_done, b.count(T, T))
                V.tensor_scalar(dn_tmp[:, 0, :], deg[:, :], LEAST, None, ALU.max).then_inc(dn_step, 1)
                dve.wait_ge(dn_step, b.count(N_STEPS, 1))
                V.reciprocal(dn_tmp[:, 1, :], dn_tmp[:, 0, :]).then_inc(dn_step, 1)
                dve.wait_ge(dn_step, b.count(N_STEPS, 2))
                V.scalar_tensor_tensor(out=dn_tmp[:, 2, :], in0=deg[:, :], scalar=0.0, in1=dn_tmp[:, 1, :],
                                       op0=ALU.is_gt, op1=ALU.mult).then_inc(dn_step, 1)
                dve.wait_ge(dn_step, b.count(N_STEPS, 3))
                V.tensor_scalar(dn1[:, b.slot, :], dn_tmp[:, 2, :], wr[:, 4:5], None, ALU.mult).then_inc(dn_step, 1)
                V.tensor_scalar(dn2[:, b.slot, :], dn_tmp[:, 2, :], wr[:, 5:6], None, ALU.mult).then_inc(dn_step, 1)

            def b_lo(b, j):
                dve.wait_ge(pt_hi, b.count(4, j + 1))
                dt, half = j % 2, j // 2
                cols = slice(BANK * half, BANK * (half + 1))
                V.scalar_tensor_tensor(out=pt[:, dt, LO, cols], in0=wide[j][:, :], scalar=PT_SCALE,
                                       in1=pt[:, dt, HI, cols], op0=ALU.mult, op1=ALU.subtract).then_inc(pt_ready, 1)

            def phase_b(b, bx):
                if bx is not None:
                    x_stats(bx)
                b_lo(b, 0)
                if bx is not None:
                    inverse_root(x_ln, x_step, bx, X_STEPS, 1.0)
                    x_normalise(bx, 0)
                    x_normalise(bx, 1)
                    h0_lo(bx, 0)
                b_lo(b, 1)
                if bx is not None:
                    x_normalise(bx, 2)
                    h0_lo(bx, 1)
                    x_normalise(bx, 3)
                    h0_lo(bx, 2)
                b_lo(b, 2)
                if bx is not None:
                    h0_lo(bx, 3)
                b_lo(b, 3)

            def phase_c(b):
                if isinstance(b.loop, int) and b.offset == 0:
                    dve.wait_ge(rows_loaded, 32)
                for t in range(T + 1):
                    if t < T:
                        dve.wait_ge(c_done, b.count(T, t + 1))
                        if t == 0:
                            dve.wait_ge(dn_step, b.count(N_STEPS, N_STEPS))
                            wait_reuse(dve, zt_done, b.count(T, 0))
                        V.scalar_tensor_tensor(out=z[:, t, :], in0=wide[t % 4][:, :], scalar=dn1[:, b.slot, t:t + 1],
                                               in1=b1_row[:, :], op0=ALU.mult, op1=ALU.add).then_inc(c_drained, 1)
                    if t >= 1:
                        dve.wait_ge(z_relu, b.count(T, t))
                        V.bn_stats(stat[:, t - 1, :], z[:, t - 1, :]).then_inc(z_stat, 1)
                variance(z_ln, z_stat, z_step, b, Z_STEPS, DH)

            def z_normalise(b, t):
                if t == 0:
                    dve.wait_ge(z_step, b.count(Z_STEPS, Z_STEPS))
                V.tensor_scalar(z[:, t, :], z[:, t, :], z_ln[:, 5, t:t + 1], z_ln[:, 4, t:t + 1],
                                ALU.subtract, ALU.mult).then_inc(zn_ready, 1)

            def phase_d(b):
                def turn_lo(t):
                    dve.wait_ge(zt_hi, b.count(T, t + 1))
                    V.tensor_tensor(zt[:, t % ZRING, LO, :], wide[t % 4][:, :], zt[:, t % ZRING, HI, :],
                                    ALU.subtract).then_inc(zt_ready, 1)

                def add_bias(t):
                    dve.wait_ge(d_done, b.count(T, t + 1))
                    if t >= 2:
                        dve.wait_ge(xw_ready, b.count(T, t - 1))
                    V.scalar_tensor_tensor(out=xf[:, t % 2, :], in0=narrow[t % 4][:, 0:DOUT], scalar=XW_SCALE,
                                           in1=bw_row[:, :], op0=ALU.mult, op1=ALU.add).then_inc(xf_ready, 1)

                def xw_lo(t):
                    dve.wait_ge(xw_hi, b.count(T, t + 1))
                    V.tensor_tensor(xw[:, t, LO, :], xf[:, t % 2, :], xw[:, t, HI, :],
                                    ALU.subtract).then_inc(xw_ready, 1)

                for t in range(3):
                    turn_lo(t)
                for t in range(T):
                    add_bias(t)
                    if t + 3 < T:
                        turn_lo(t + 3)
                    xw_lo(t)

            def phase_e(b, bd):
                for et in range(T):
                    dve.wait_ge(t2_hi, b.count(T, et + 1))
                    V.scalar_tensor_tensor(out=edge[:, et, LO, :], in0=narrow[et % 4][:, 0:DOUT],
                                           scalar=be[:, b.slot, et:et + 1], in1=edge[:, et, HI, :],
                                           op0=ALU.mult, op1=ALU.subtract).then_inc(t2_ready, 1)
                    if bd is not None:
                        degree(bd, et)

            def phase_f(b, bi, bz):
                if bz is not None:
                    inverse_root(z_ln, z_step, bz, Z_STEPS, ZN_SCALE)
                for ct in range(T):
                    if bi is not None and ct % 2 == 0:
                        incidence(bi, ct // 2)
                    dve.wait_ge(f_done, b.count(T, ct + 1))
                    if ct == 0:
                        dve.wait_ge(res_ready, b.count(1, 1))
                    V.scalar_tensor_tensor(out=res[:, b.slot, ct, :], in0=narrow[ct % 4][:, 0:DOUT],
                                           scalar=dn2[:, b.slot, ct:ct + 1], in1=res[:, b.slot, ct, :],
                                           op0=ALU.mult, op1=ALU.add).then_inc(out_ready, 1)
                    if bz is not None:
                        z_normalise(bz, ct)

            def phase_a(b):
                for et in range(T):
                    dve.wait_ge(a_done, b.count(T, et + 1))
                    V.tensor_scalar(be_cnt[:, et:et + 1], narrow[et % 4][:, ONE:ONE + 1], 1.0, None,
                                    ALU.max).then_inc(be_step, 1)
                    dve.wait_ge(be_step, b.count(2 * T, 2 * et + 1))
                    V.reciprocal(be[:, b.slot, et:et + 1], be_cnt[:, et:et + 1]).then_inc(be_step, 1)
                    dve.wait_ge(t1_hi, b.count(T, et + 1))
                    V.scalar_tensor_tensor(out=edge[:, et, LO, :], in0=narrow[et % 4][:, 0:DIN],
                                           scalar=be[:, b.slot, et:et + 1], in1=edge[:, et, HI, :],
                                           op0=ALU.mult, op1=ALU.subtract).then_inc(t1_ready, 1)
                node_inverse(b)

            def extremes(src, rest, i):
                for sign in range(2):
                    if i + sign > 0:
                        dve.wait_ge(max_step, 2 * i + sign)
                    V.tensor_scalar(rest, src, 1.0 - 2.0 * sign, None, ALU.mult, ALU.max,
                                    accum_out=wext[:, i, sign:sign + 1]).then_inc(max_step, 1)

            dve.wait_ge(weights_loaded, 64)
            for ht in range(HT_):
                last = V.tensor_copy(beta_cols[:, ht, :], gb[:, 1, ht:ht + 1].to_broadcast([P, P]))
            last.then_inc(beta_ready, 1)
            for ht in range(HT_):
                last = V.tensor_scalar(gf[:, ht, :], w2f[:, ht, :], gb[:, 0, ht:ht + 1], None, ALU.mult)
            last.then_inc(setup_step, 1)
            extremes(w1f, junk[:, :], 0)
            dve.wait_ge(setup_step, 1)
            extremes(gf, junk[:, :], 1)
            dve.wait_ge(bias_done, 1)
            extremes(wide[3][:, 0:DOUT], junk[:, 0:DOUT], 2)
            dve.wait_ge(max_step, 6)
            V.tensor_reduce(wm[:, 0:3], wext[:, :, :], mybir.AxisListType.X, ALU.max).then_inc(setup_step, 1)
            dve.wait_ge(setup_step, 2)
            V.scalar_tensor_tensor(out=wm[:, 1:2], in0=wm[:, 2:3], scalar=BIAS_ROOM, in1=wm[:, 1:2],
                                   op0=ALU.mult, op1=ALU.max).then_inc(max_here, 1)
            x_stats(Batch(0, 0))
            inverse_root(x_ln, x_step, Batch(0, 0), X_STEPS, 1.0)
            x_normalise(Batch(0, 0), 0)
            x_normalise(Batch(0, 0), 1)
            h0_lo(Batch(0, 0), 0)
            x_normalise(Batch(0, 0), 2)
            h0_lo(Batch(0, 0), 1)
            x_normalise(Batch(0, 0), 3)
            h0_lo(Batch(0, 0), 2)
            h0_lo(Batch(0, 0), 3)
            dve.wait_ge(max_all, 1)
            V.tensor_scalar(wall[:, :], wall[:, :], TINY, None, ALU.max).then_inc(setup_step, 1)
            dve.wait_ge(setup_step, 3)
            V.tensor_scalar(wp[:, :].bitcast(U32), wall[:, :].bitcast(U32), EXPONENT, None,
                            ALU.bitwise_and).then_inc(setup_step, 1)
            dve.wait_ge(setup_step, 4)
            V.reciprocal(wr[:, 0:2], wp[:, :])
            V.tensor_scalar(wr[:, 4:5], wp[:, 0:1], 1.0 / (H0_SCALE * PT_SCALE * W_SCALE), None, ALU.mult)
            V.tensor_scalar(wr[:, 5:6], wp[:, 1:2], 1.0 / (ZN_SCALE * W_SCALE * XW_SCALE), None,
                            ALU.mult).then_inc(setup_step, 1)
            dve.wait_ge(setup_step, 5)
            V.tensor_scalar(w1f, w1f, wr[:, 0:1], W_SCALE, ALU.mult, ALU.mult).then_inc(setup_step, 1)
            V.tensor_scalar(gf, gf, wr[:, 1:2], W_SCALE, ALU.mult, ALU.mult).then_inc(setup_step, 1)
            V.tensor_scalar(bw_row[:, :], wide[3][:, 0:DOUT], wr[:, 1:2], ZN_SCALE * W_SCALE * XW_SCALE,
                            ALU.mult, ALU.mult).then_inc(setup_step, 1)
            dve.wait_ge(w_hi, 1)
            V.tensor_tensor(w1s[:, :, LO, :], w1f, w1s[:, :, HI, :], ALU.subtract).then_inc(w_ready, 1)
            dve.wait_ge(w_hi, 2)
            V.tensor_tensor(w2s[:, :, LO, :], gf, w2s[:, :, HI, :], ALU.subtract).then_inc(w_ready, 1)
            for q in range(QUARTERS):
                incidence(Batch(0, 0), q)
            for ct in range(T):
                degree(Batch(0, 0), ct)
            phase_a(Batch(0, 0))
            phase_b(Batch(0, 0), Batch(0, 1))
            for ct in range(T):
                if ct % 2 == 0:
                    incidence(Batch(0, 1), ct // 2)
                degree(Batch(0, 1), ct)
            phase_c(Batch(0, 0))
            inverse_root(z_ln, z_step, Batch(0, 0), Z_STEPS, ZN_SCALE)
            for t in range(T):
                z_normalise(Batch(0, 0), t)
            phase_a(Batch(0, 1))
            with dve.Fori(0, N - 2, 2) as n:
                for k in range(2):
                    phase_d(Batch(n, k))
                    phase_b(Batch(n, k + 1), Batch(n, k + 2))
                    phase_e(Batch(n, k), Batch(n, k + 2))
                    phase_c(Batch(n, k + 1))
                    phase_f(Batch(n, k), Batch(n, k + 2), Batch(n, k + 1))
                    phase_a(Batch(n, k + 2))
            phase_d(Batch(0, N - 2))
            phase_b(Batch(0, N - 1), None)
            phase_e(Batch(0, N - 2), None)
            phase_c(Batch(0, N - 1))
            phase_f(Batch(0, N - 2), None, Batch(0, N - 1))
            phase_d(Batch(0, N - 1))
            phase_e(Batch(0, N - 1), None)
            phase_f(Batch(0, N - 1), None, None)
    return nc


def kernel(x, adj, L0_gnn_W1, L0_gnn_b1, L0_gnn_gamma, L0_gnn_beta, L0_gnn_W2, L0_gnn_b2):
    import numpy as np
    import concourse.bacc as bacc
    from concourse.bass_utils import run_bass_kernel_spmd as run

    arrays = {
        "x": np.ascontiguousarray(x),
        "adj": np.ascontiguousarray(adj),
        "w1t": np.ascontiguousarray(np.transpose(L0_gnn_W1)),
        "b1": np.ascontiguousarray(np.reshape(L0_gnn_b1, (1, -1))),
        "gamma": np.ascontiguousarray(np.transpose(np.reshape(L0_gnn_gamma, (-1, P)))),
        "beta": np.ascontiguousarray(np.transpose(np.reshape(L0_gnn_beta, (-1, P)))),
        "w2t": np.ascontiguousarray(np.transpose(L0_gnn_W2)),
        "b2": np.ascontiguousarray(np.reshape(L0_gnn_b2, (1, -1))),
    }
    nc = bacc.Bacc("TRN2", target_bir_lowering=False, num_devices=1)
    ins = [nc.dram_tensor(name, a.shape, mybir.dt.from_np(a.dtype), kind="ExternalInput").ap()
           for name, a in arrays.items()]
    out = nc.dram_tensor("out", arrays["x"].shape, F32, kind="ExternalOutput").ap()
    hypergraph_block(nc, *ins, out)
    return run(nc, [arrays], core_ids=[0]).results[0]["out"]
```

```python
from contextlib import ExitStack

import concourse.bass as bass
from concourse import mybir

ALU = mybir.AluOpType
ACT = mybir.ActivationFunctionType
RMAX = bass.bass_isa.ReduceOp.max
F32 = mybir.dt.float32
F16 = mybir.dt.float16
BF16 = mybir.dt.bfloat16
U32 = mybir.dt.uint32

P = 128
BANK = 512
HI, LO = 0, 1

H0_SCALE = 2.0 ** 8
PT_SCALE = 2.0 ** -7
W_SCALE = 2.0 ** 8
ZN_SCALE = 2.0 ** 4
XW_SCALE = 2.0 ** -7
BIAS_ROOM = 2.0 ** -8
TINY = 2.0 ** -100
LEAST = 2.0 ** -126
EXPONENT = 0x7F800000
EPS = 1e-5


class Batch:

    def __init__(self, loop, offset):
        self.loop, self.offset, self.slot = loop, offset, offset % 2

    def next(self, k):
        return Batch(self.loop, self.offset + k)

    def index(self):
        return self.loop + self.offset

    def count(self, per_batch, more):
        return self.loop * per_batch + (self.offset * per_batch + more)


def wait_reuse(eng, sem, value):
    if not (isinstance(value, int) and value <= 0):
        eng.wait_ge(sem, value)


def hypergraph_block(nc, x, adj, w1t, b1, gamma, beta, w2t, b2, out):
    N, C, DIN = x.shape
    DH = w1t.shape[1]
    DOUT = w2t.shape[1]
    T = C // P
    DT = DIN // P
    HT_ = DH // P
    assert C == 1024 and T == 8 and DIN == DOUT == 256 and DH == BANK and N % 2 == 0 and N >= 4
    ONE = DIN
    LO_AT = DIN + 8
    HL = LO_AT + DIN
    GROUPS = 4
    GT = T // GROUPS
    QUARTERS = 4
    QT = T // QUARTERS
    X_STEPS, Z_STEPS, N_STEPS = 11, 11, 5
    ZRING = 6

    with ExitStack() as ctx:
        def sb(name, shape, dt=F32):
            return ctx.enter_context(nc.sbuf_tensor(name, shape, dt))

        def sem(name):
            return ctx.enter_context(nc.semaphore(name))

        adj_in = sb("adj_in", [P, T, C])
        inc = sb("incidence", [P, 2, T, C], BF16)
        inc_t = sb("incidence_t", [P, 2, T, T, P], BF16)
        x_in = sb("x_in", [P, T, DIN])
        u = sb("h0_ring", [P, 2, GT, DIN])
        h0 = sb("h0_split", [P, T, HL], F16)
        res = sb("residual", [P, 2, T, DOUT])
        edge = sb("edge_means", [P, T, 2, DIN], F16)
        pt = sb("pt_split", [P, DT, 2, C], F16)
        z = sb("z", [P, T, DH])
        zt = z[:, :, :].bitcast(F16).rearrange("p t (k c) -> p t k c", c=P)
        zs = sb("z_split_ring", [P, ZRING, 2, DH], F16)
        xw = sb("xw_split", [P, T, 2, DOUT], F16)
        xf = sb("xw_ring", [P, 2, DOUT])
        w1s = sb("w1_split", [P, DT, 2, DH], F16)
        w2s = sb("w2_split", [P, HT_, 2, DOUT], F16)
        b1_row = sb("b1_row", [P, DH])
        b2_row = sb("b2_row", [P, DOUT])
        bw_row = sb("bias_w2_row", [P, DOUT])
        edge_w = sb("edge_weights", [P, C])
        junk = sb("junk", [P, C])
        stat = sb("stat", [P, T, 6])
        x_ln = sb("x_ln", [P, 7, T])
        z_ln = sb("z_ln", [P, 7, T])
        deg = sb("node_degree", [P, T])
        dn_tmp = sb("dn_tmp", [P, 3, T])
        dn1 = sb("dn_conv1", [P, 2, T])
        dn2 = sb("dn_conv2", [P, 2, T])
        be_cnt = sb("edge_count", [P, T])
        be = sb("edge_inverse", [P, 2, T])
        gb = sb("gamma_beta", [P, 2, HT_])
        wm = sb("weight_max", [P, 4])
        wext = sb("weight_extremes", [P, 3, 2])
        wall = sb("weight_max_all", [P, 2])
        wp = sb("weight_power", [P, 2])
        wr = sb("weight_factor", [P, 6])
        w1f = z[:, 0:2, :]
        w2f = z[:, 2:4, :].rearrange("p a (b o) -> p (a b) o", o=DOUT)
        gf = z[:, 4:6, :].rearrange("p a (b o) -> p (a b) o", o=DOUT)
        beta_cols = z[:, 6, :].rearrange("p (t m) -> p t m", m=P)

        narrow = [ctx.enter_context(nc.psum_tensor(f"narrow{i}", [P, BANK], F32)) for i in range(4)]
        wide = [ctx.enter_context(nc.psum_tensor(f"wide{i}", [P, BANK], F32)) for i in range(4)]

        x_loaded = sem("x_loaded")
        w_loaded = sem("w_loaded")
        adj_loaded = [sem(f"adj_loaded{q}") for q in range(QUARTERS)]
        weights_loaded = sem("weights_loaded")
        rows_loaded = sem("rows_loaded")
        stored = [sem(f"stored{q}") for q in range(QUARTERS)]
        ones_set = sem("ones_set")
        max_here = sem("max_here")
        max_all = sem("max_all")
        setup_step = sem("setup_step")
        max_step = sem("max_step")
        beta_ready = sem("beta_ready")
        bias_done = sem("bias_done")
        bias_read = sem("bias_read")
        w_hi = sem("w_hi")
        w_ready = sem("w_ready")
        x_stat = sem("x_stat")
        x_step = sem("x_step")
        u_ready = sem("u_ready")
        h0_hi = sem("h0_hi")
        h0_ready = sem("h0_ready")
        x_added = sem("x_added")
        res_ready = sem("res_ready")
        inc_ready = sem("inc_ready")
        deg_done = sem("deg_done")
        dn_step = sem("dn_step")
        a_done = sem("a_done")
        be_step = sem("be_step")
        t1_hi = sem("t1_hi")
        t1_ready = sem("t1_ready")
        inc_t_ready = [sem(f"inc_t_ready{q}") for q in range(QUARTERS)]
        b_done = sem("b_done")
        pt_hi = sem("pt_hi")
        pt_ready = sem("pt_ready")
        c_done = sem("c_done")
        c_drained = sem("c_drained")
        z_relu = sem("z_relu")
        z_stat = sem("z_stat")
        z_step = sem("z_step")
        zs_hi = sem("zs_hi")
        zs_ready = sem("zs_ready")
        zt_ready = [sem(f"zt_ready{q}") for q in range(QUARTERS)]
        d_done = sem("d_done")
        xf_ready = sem("xf_ready")
        xw_hi = sem("xw_hi")
        xw_ready = sem("xw_ready")
        e_done = sem("e_done")
        t2_hi = sem("t2_hi")
        t2_ready = sem("t2_ready")
        f_done = sem("f_done")
        out_ready = sem("out_ready")

        def rows(ap, b):
            if isinstance(b.loop, int):
                part = ap[b.offset:b.offset + 1]
            else:
                part = ap[bass.ds(b.index(), 1)]
            return part.rearrange("b (p t) d -> p (b t) d", t=T)

        block = ctx.enter_context(nc.Block())

        @block.sync
        def _(sp):
            def load_x(b):
                wait_reuse(sp, res_ready, b.count(1, 0))
                sp.dma_start(x_in[:, :, :], rows(x, b)).then_inc(x_loaded, 16)

            def load_adj(b, q):
                wait_reuse(sp, inc_ready, b.count(T, QT * (q + 1) - T))
                wait_reuse(sp, deg_done, b.count(T, QT * (q + 1) - T))
                sp.dma_start(adj_in[:, QT * q:QT * (q + 1), :],
                             rows(adj, b)[:, QT * q:QT * (q + 1), :]).then_inc(adj_loaded[q], 16)

            def load_edge_weights(b):
                wait_reuse(sp, deg_done, b.count(T, 0))
                if isinstance(b.loop, int):
                    first = adj[b.offset:b.offset + 1, 0, :]
                else:
                    first = adj[bass.ds(b.index(), 1), 0, :]
                sp.dma_start(edge_w[:, :], first.to_broadcast([P, C])).then_inc(w_loaded, 16)

            def transpose_inc(b, q):
                ts = slice(QT * q, QT * (q + 1))
                sp.dma_start_transpose(inc_t[:, b.slot, ts, :, :].rearrange("p a k c -> p (a k) c"),
                                       inc[:, b.slot, ts, :].rearrange("p a e -> p (a e)")).then_inc(inc_t_ready[q], 16)

            def transpose_z(b, q):
                slot = QT * q % ZRING
                sp.dma_start_transpose(zt[:, QT * q:QT * (q + 1), :, :].rearrange("p a k c -> p (a k) c"),
                                       zs[:, slot:slot + QT, :, :].rearrange("p a b h -> p (a b h)")).then_inc(zt_ready[q], 16)

            def store(b, q):
                ts = slice(QT * q, QT * (q + 1))
                sp.dma_start(rows(out, b)[:, ts, :], res[:, b.slot, ts, :]).then_inc(stored[q], 16)

            def step(b, load=True, turn_h=True, turn_z=True):
                for q in range(QUARTERS):
                    if turn_z:
                        sp.wait_ge(zs_ready, b.count(T, T + QT * (q + 1)))
                    if turn_h and q == QUARTERS - 1:
                        sp.wait_ge(inc_ready, b.count(QUARTERS, 3 * QUARTERS) * QT)
                    sp.wait_ge(out_ready, b.count(QUARTERS, q + 1) * QT)
                    store(b, q)
                    if turn_z:
                        transpose_z(b.next(1), q)
                if turn_h:
                    for q in range(QUARTERS):
                        transpose_inc(b.next(2), q)
                if load:
                    load_x(b.next(3))
                    for q in range(QUARTERS):
                        load_adj(b.next(3), q)
                    load_edge_weights(b.next(3))

            load_x(Batch(0, 0))
            sp.dma_start(w2f, w2t.rearrange("(t p) o -> p t o", p=P)).then_inc(weights_loaded, 16)
            sp.dma_start(gb[:, 0, :], gamma).then_inc(weights_loaded, 16)
            sp.dma_start(gb[:, 1, :], beta).then_inc(weights_loaded, 16)
            sp.dma_start(w1f, w1t.rearrange("(t p) h -> p t h", p=P)).then_inc(weights_loaded, 16)
            for q in range(QUARTERS):
                load_adj(Batch(0, 0), q)
            load_edge_weights(Batch(0, 0))
            sp.dma_start(b2_row[:, :], b2.to_broadcast([P, DOUT])).then_inc(rows_loaded, 16)
            sp.dma_start(b1_row[:, :], b1.to_broadcast([P, DH])).then_inc(rows_loaded, 16)
            for q in range(QUARTERS):
                sp.wait_ge(inc_ready, QT * (q + 1))
                transpose_inc(Batch(0, 0), q)
            load_x(Batch(0, 1))
            for q in range(QUARTERS):
                load_adj(Batch(0, 1), q)
            load_edge_weights(Batch(0, 1))
            for q in range(QUARTERS):
                sp.wait_ge(inc_ready, T + QT * (q + 1))
                transpose_inc(Batch(0, 1), q)
            for q in range(QUARTERS):
                sp.wait_ge(zs_ready, QT * (q + 1))
                transpose_z(Batch(0, 0), q)
            load_x(Batch(0, 2))
            for q in range(QUARTERS):
                load_adj(Batch(0, 2), q)
            load_edge_weights(Batch(0, 2))
            with sp.Fori(0, N - 5, 2) as n:
                for k in range(2):
                    step(Batch(n, k))
            step(Batch(0, N - 4))
            step(Batch(0, N - 3), load=False)
            step(Batch(0, N - 2), load=False, turn_h=False)
            step(Batch(0, N - 1), load=False, turn_h=False, turn_z=False)
            for q in range(QUARTERS):
                sp.wait_ge(stored[q], 16 * N)

        @block.gpsimd
        def _(pool):
            nc.gpsimd.memset(h0[:, :, ONE:ONE + 1], 1.0).then_inc(ones_set, 1)

            def residual(b):
                for g in range(GROUPS):
                    pool.wait_ge(u_ready, b.count(T, GT * (g + 1)))
                    xs = x_in[:, GT * g:GT * (g + 1), :]
                    nc.gpsimd.tensor_tensor(xs, xs, u[:, g % 2, :, :], ALU.add).then_inc(x_added, 1)
                pool.wait_ge(x_added, b.count(GROUPS, GROUPS))
                if isinstance(b.loop, int) and b.offset == 0:
                    pool.wait_ge(rows_loaded, 32)
                for q in range(QUARTERS):
                    wait_reuse(pool, stored[q], b.count(16, -16))
                nc.gpsimd.tensor_tensor(res[:, b.slot, :, :], x_in[:, :, :],
                                        b2_row[:, None, :].to_broadcast([P, T, DOUT]),
                                        ALU.add).then_inc(res_ready, 1)

            residual(Batch(0, 0))
            pool.wait_ge(max_here, 1)
            nc.gpsimd.partition_all_reduce(wall[:, :], wm[:, 0:2], P, RMAX).then_inc(max_all, 1)
            residual(Batch(0, 1))
            with pool.Fori(0, N - 2, 2) as n:
                for k in range(2):
                    residual(Batch(n, k + 2))

        @block.tensor
        def _(pe):
            def take_narrow(b, t, own, before, b_before):
                if t >= 4:
                    pe.wait_ge(own, b.count(T, t - 3))
                elif b_before is not None:
                    pe.wait_ge(before, b_before.count(T, t + 5))
                return narrow[t % 4]

            def first_stage_a():
                b = Batch(0, 0)
                pe.wait_ge(ones_set, 1)
                for ct in range(T):
                    pe.wait_ge(inc_ready, ct + 1)
                    if ct % GT == 0:
                        pe.wait_ge(h0_ready, ct // GT + 1)
                    for et in range(T):
                        acc = (narrow + wide)[et]
                        cols = slice(P * et, P * (et + 1))
                        nc.tensor.matmul(acc[:, 0:ONE + 1], inc[:, b.slot, ct, cols], h0[:, ct, 0:ONE + 1],
                                         start=(ct == 0), stop=False)
                        last = nc.tensor.matmul(acc[:, 0:DIN], inc[:, b.slot, ct, cols], h0[:, ct, LO_AT:HL],
                                                start=False, stop=(ct == T - 1))
                        if ct == T - 1:
                            last.then_inc(a_done, 1)

            def stage_a(b):
                opening = isinstance(b.loop, int) and b.offset < 2
                pe.wait_ge(inc_ready, b.count(T, T))
                pe.wait_ge(h0_ready, b.count(GROUPS, GROUPS))
                for et in range(T):
                    if opening:
                        acc = take_narrow(b, et, t1_ready, t1_ready, None)
                    else:
                        acc = take_narrow(b, et, t1_ready, out_ready, b.next(-2))
                    cols = slice(P * et, P * (et + 1))
                    for ct in range(T):
                        nc.tensor.matmul(acc[:, 0:ONE + 1], inc[:, b.slot, ct, cols], h0[:, ct, 0:ONE + 1],
                                         start=(ct == 0), stop=False)
                        last = nc.tensor.matmul(acc[:, 0:DIN], inc[:, b.slot, ct, cols], h0[:, ct, LO_AT:HL],
                                                start=False, stop=(ct == T - 1))
                    last.then_inc(a_done, 1)

            def stage_b(b):
                for q in range(QUARTERS):
                    pe.wait_ge(inc_t_ready[q], b.count(16, 16))
                for j in range(4):
                    dt, half = j % 2, j // 2
                    if isinstance(b.loop, int) and b.offset == 0:
                        pe.wait_ge(t1_ready, 5 + j)
                    else:
                        pe.wait_ge(c_drained, b.count(T, 5 + j - T))
                    for et in range(T):
                        if j == 0:
                            pe.wait_ge(t1_ready, b.count(T, et + 1))
                        for part in (HI, LO):
                            last = nc.tensor.matmul(wide[j][:, :], edge[:, et, part, P * dt:P * (dt + 1)],
                                                    inc_t[:, b.slot, 4 * half:4 * (half + 1), et, :],
                                                    start=(et == 0 and part == HI), stop=(et == T - 1 and part == LO))
                    last.then_inc(b_done, 1)

            def stage_c(b):
                if isinstance(b.loop, int) and b.offset == 0:
                    pe.wait_ge(w_ready, 1)
                for t in range(T):
                    pe.wait_ge(pt_ready, b.count(4, max(2 * (t // 4 + 1), min(t + 1, 4))))
                    if t >= 4:
                        pe.wait_ge(c_drained, b.count(T, t - 3))
                    k = 0
                    for dt in range(DT):
                        for left, right in ((HI, HI), (HI, LO), (LO, HI)):
                            last = nc.tensor.matmul(wide[t % 4][:, :], pt[:, dt, left, P * t:P * (t + 1)],
                                                    w1s[:, dt, right, :], start=(k == 0), stop=(k == 3 * DT - 1))
                            k += 1
                    last.then_inc(c_done, 1)

            def stage_d(b):
                final = isinstance(b.loop, int) and b.offset == N - 1
                if isinstance(b.loop, int) and b.offset == 0:
                    pe.wait_ge(w_ready, 2)
                for t in range(T):
                    if final:
                        acc = take_narrow(b, t, xf_ready, out_ready, b.next(-1))
                    else:
                        acc = take_narrow(b, t, xf_ready, t1_ready, b.next(1))
                    if t % QT == 0:
                        pe.wait_ge(zt_ready[t // QT], b.count(16, 16))
                    k = 0
                    for ht in range(HT_):
                        for left, right in ((HI, HI), (HI, LO), (LO, HI)):
                            last = nc.tensor.matmul(acc[:, 0:DOUT], zt[:, t, HT_ * left + ht, :],
                                                    w2s[:, ht, right, :], start=(k == 0), stop=(k == 3 * HT_ - 1))
                            k += 1
                    last.then_inc(d_done, 1)

            def stage_e(b):
                for et in range(T):
                    acc = take_narrow(b, et, t2_ready, xf_ready, b)
                    for ct in range(T):
                        if et == 0:
                            pe.wait_ge(xw_ready, b.count(T, ct + 1))
                        for part in (HI, LO):
                            last = nc.tensor.matmul(acc[:, 0:DOUT], inc[:, b.slot, ct, P * et:P * (et + 1)],
                                                    xw[:, ct, part, :],
                                                    start=(ct == 0 and part == HI), stop=(ct == T - 1 and part == LO))
                    last.then_inc(e_done, 1)

            def stage_f(b):
                for ct in range(T):
                    acc = take_narrow(b, ct, out_ready, t2_ready, b)
                    for et in range(T):
                        if ct == 0:
                            pe.wait_ge(t2_ready, b.count(T, et + 1))
                        for part in (HI, LO):
                            last = nc.tensor.matmul(acc[:, 0:DOUT], inc_t[:, b.slot, ct, et, :],
                                                    edge[:, et, part, :],
                                                    start=(et == 0 and part == HI), stop=(et == T - 1 and part == LO))
                    last.then_inc(f_done, 1)

            pe.wait_ge(beta_ready, 1)
            for ht in range(HT_):
                last = nc.tensor.matmul(narrow[3][:, 0:DOUT], beta_cols[:, ht, :], w2f[:, ht, :],
                                        start=(ht == 0), stop=(ht == HT_ - 1))
            last.then_inc(bias_done, 1)
            pe.wait_ge(bias_read, 1)
            first_stage_a()
            stage_b(Batch(0, 0))
            stage_c(Batch(0, 0))
            stage_a(Batch(0, 1))
            with pe.Fori(0, N - 2, 2) as n:
                for k in range(2):
                    stage_d(Batch(n, k))
                    stage_b(Batch(n, k + 1))
                    stage_e(Batch(n, k))
                    stage_c(Batch(n, k + 1))
                    stage_f(Batch(n, k))
                    stage_a(Batch(n, k + 2))
            stage_d(Batch(0, N - 2))
            stage_b(Batch(0, N - 1))
            stage_e(Batch(0, N - 2))
            stage_c(Batch(0, N - 1))
            stage_f(Batch(0, N - 2))
            stage_d(Batch(0, N - 1))
            stage_e(Batch(0, N - 1))
            stage_f(Batch(0, N - 1))

        @block.scalar
        def _(act):
            def copy(o, i, **kw):
                return nc.scalar.activation(o, i, ACT.Copy, **kw)

            def root_x(b):
                act.wait_ge(x_step, b.count(X_STEPS, 4))
                nc.scalar.activation(x_ln[:, 1, :], x_ln[:, 0, :], ACT.Sqrt).then_inc(x_step, 1)

            def h0_tiles(b, g):
                if g == 0:
                    act.wait_ge(x_step, b.count(X_STEPS, X_STEPS))
                wait_reuse(act, x_added, b.count(GROUPS, g - 1))
                wait_reuse(act, h0_ready, b.count(GROUPS, g - 1))
                for i in range(GT):
                    t = GT * g + i
                    nc.scalar.activation(u[:, g % 2, i, :], x_in[:, t, :], ACT.Relu, scale=x_ln[:, 4, t:t + 1],
                                         bias=x_ln[:, 6, t:t + 1]).then_inc(u_ready, 1)

            def h0_hi_part(b, g):
                act.wait_ge(u_ready, b.count(T, GT * (g + 1)))
                if g == 0:
                    wait_reuse(act, a_done, b.count(T, 0))
                copy(h0[:, GT * g:GT * (g + 1), 0:DIN], u[:, g % 2, :, :], scale=H0_SCALE).then_inc(h0_hi, 1)

            def z_split(b, t):
                if t == 0:
                    act.wait_ge(z_step, b.count(Z_STEPS, Z_STEPS))
                if t % QT == 0:
                    if t >= ZRING:
                        act.wait_ge(zt_ready[(t - ZRING) // QT], b.count(16, 16))
                    else:
                        wait_reuse(act, zt_ready[(t if t + ZRING >= T else t + ZRING) // QT], b.count(16, 0))
                by = dict(scale=z_ln[:, 4, t:t + 1], bias=z_ln[:, 6, t:t + 1])
                nc.scalar.activation(zs[:, t % ZRING, HI, :], z[:, t, :], ACT.Identity, **by)
                nc.scalar.activation(z[:, t, :], z[:, t, :], ACT.Identity, **by).then_inc(zs_hi, 1)

            def drain_b(b, j):
                act.wait_ge(b_done, b.count(4, j + 1))
                if j == 0:
                    wait_reuse(act, c_done, b.count(T, 0))
                dt, half = j % 2, j // 2
                copy(pt[:, dt, HI, BANK * half:BANK * (half + 1)], wide[j][:, :], scale=PT_SCALE).then_inc(pt_hi, 1)

            def phase_b(b, bx):
                drain_b(b, 0)
                if bx is not None:
                    root_x(bx)
                    h0_tiles(bx, 0)
                    h0_tiles(bx, 1)
                    h0_hi_part(bx, 0)
                drain_b(b, 1)
                if bx is not None:
                    h0_hi_part(bx, 1)
                    h0_tiles(bx, 2)
                    h0_tiles(bx, 3)
                    h0_hi_part(bx, 2)
                drain_b(b, 2)
                if bx is not None:
                    h0_hi_part(bx, 3)
                drain_b(b, 3)

            def z_relus(b):
                for t in range(T):
                    act.wait_ge(c_drained, b.count(T, t + 1))
                    nc.scalar.activation(z[:, t, :], z[:, t, :], ACT.Relu).then_inc(z_relu, 1)
                act.wait_ge(z_step, b.count(Z_STEPS, 4))
                nc.scalar.activation(z_ln[:, 1, :], z_ln[:, 0, :], ACT.Sqrt).then_inc(z_step, 1)

            def phase_c(b):
                z_relus(b)
                for t in range(T):
                    z_split(b, t)

            def phase_d(b):
                for t in range(T):
                    act.wait_ge(xf_ready, b.count(T, t + 1))
                    copy(xw[:, t, HI, :], xf[:, t % 2, :]).then_inc(xw_hi, 1)

            def phase_e(b):
                if isinstance(b.loop, int) and b.offset == N - 1:
                    act.wait_ge(f_done, b.count(T, 0))
                else:
                    act.wait_ge(b_done, b.count(4, 8))
                for et in range(T):
                    act.wait_ge(e_done, b.count(T, et + 1))
                    copy(edge[:, et, HI, :], narrow[et % 4][:, 0:DOUT], scale=be[:, b.slot, et:et + 1]).then_inc(t2_hi, 1)

            def t1_hi_part(b, et):
                act.wait_ge(be_step, b.count(2 * T, 2 * et + 2))
                bank = (narrow + wide)[et] if isinstance(b.loop, int) and b.offset == 0 else narrow[et % 4]
                copy(edge[:, et, HI, :], bank[:, 0:DIN], scale=be[:, b.slot, et:et + 1]).then_inc(t1_hi, 1)

            def phase_a(b):
                act.wait_ge(f_done, b.count(T, -T))
                for et in range(T):
                    t1_hi_part(b, et)

            root_x(Batch(0, 0))
            for g in range(GROUPS):
                h0_tiles(Batch(0, 0), g)
                if g >= 1:
                    h0_hi_part(Batch(0, 0), g - 1)
            h0_hi_part(Batch(0, 0), GROUPS - 1)
            act.wait_ge(setup_step, 6)
            copy(w1s[:, :, HI, :], w1f).then_inc(w_hi, 1)
            act.wait_ge(setup_step, 7)
            copy(w2s[:, :, HI, :], gf).then_inc(w_hi, 1)
            for et in range(T):
                t1_hi_part(Batch(0, 0), et)
            phase_b(Batch(0, 0), Batch(0, 1))
            z_relus(Batch(0, 0))
            act.wait_ge(b_done, 4)
            for t in range(T):
                z_split(Batch(0, 0), t)
                t1_hi_part(Batch(0, 1), t)
            with act.Fori(0, N - 2, 2) as n:
                for k in range(2):
                    phase_d(Batch(n, k))
                    phase_b(Batch(n, k + 1), Batch(n, k + 2))
                    phase_e(Batch(n, k))
                    phase_c(Batch(n, k + 1))
                    phase_a(Batch(n, k + 2))
            phase_d(Batch(0, N - 2))
            phase_b(Batch(0, N - 1), None)
            phase_e(Batch(0, N - 2))
            phase_c(Batch(0, N - 1))
            phase_d(Batch(0, N - 1))
            phase_e(Batch(0, N - 1))

        @block.vector
        def _(dve):
            V = nc.vector

            def variance(ln, stat_sem, step_sem, b, steps, n):
                s, _, y, tmp, _, mean = (ln[:, i, :] for i in range(6))
                dve.wait_ge(stat_sem, b.count(T, T))
                V.tensor_tensor(mean, stat[:, :, 1], stat[:, :, 4], ALU.add)
                V.tensor_tensor(tmp, stat[:, :, 1], stat[:, :, 4], ALU.subtract)
                V.tensor_tensor(s, stat[:, :, 2], stat[:, :, 5], ALU.add).then_inc(step_sem, 1)
                dve.wait_ge(step_sem, b.count(steps, 1))
                V.tensor_scalar(mean, mean, 0.5, None, ALU.mult)
                V.tensor_tensor(y, tmp, tmp, ALU.mult).then_inc(step_sem, 1)
                dve.wait_ge(step_sem, b.count(steps, 2))
                V.scalar_tensor_tensor(out=tmp, in0=s, scalar=4.0 / n, in1=y, op0=ALU.mult,
                                       op1=ALU.add).then_inc(step_sem, 1)
                dve.wait_ge(step_sem, b.count(steps, 3))
                V.tensor_scalar(s, tmp, 0.25, EPS, ALU.mult, ALU.add).then_inc(step_sem, 1)

            def inverse_root(ln, step_sem, b, steps, scale):
                s, root, y, tmp, rstd = (ln[:, i, :] for i in range(5))
                dve.wait_ge(step_sem, b.count(steps, 5))
                V.reciprocal(y, root).then_inc(step_sem, 1)
                dve.wait_ge(step_sem, b.count(steps, 6))
                V.tensor_tensor(tmp, y, y, ALU.mult).then_inc(step_sem, 1)
                dve.wait_ge(step_sem, b.count(steps, 7))
                V.tensor_tensor(tmp, tmp, s, ALU.mult).then_inc(step_sem, 1)
                dve.wait_ge(step_sem, b.count(steps, 8))
                V.tensor_scalar(tmp, tmp, -0.5 * scale, 1.5 * scale, ALU.mult, ALU.add).then_inc(step_sem, 1)
                dve.wait_ge(step_sem, b.count(steps, 9))
                V.tensor_tensor(rstd, tmp, y, ALU.mult).then_inc(step_sem, 1)
                dve.wait_ge(step_sem, b.count(steps, 10))
                V.scalar_tensor_tensor(out=ln[:, 6, :], in0=ln[:, 5, :], scalar=-1.0, in1=rstd, op0=ALU.mult,
                                       op1=ALU.mult).then_inc(step_sem, 1)

            def x_stats(b):
                dve.wait_ge(x_loaded, b.count(16, 16))
                for t in range(T):
                    V.bn_stats(stat[:, t, :], x_in[:, t, :]).then_inc(x_stat, 1)
                variance(x_ln, x_stat, x_step, b, X_STEPS, DIN)

            def h0_lo(b, g):
                dve.wait_ge(h0_hi, b.count(GROUPS, g + 1))
                ts = slice(GT * g, GT * (g + 1))
                V.scalar_tensor_tensor(out=h0[:, ts, LO_AT:HL], in0=u[:, g % 2, :, :], scalar=H0_SCALE,
                                       in1=h0[:, ts, 0:DIN], op0=ALU.mult, op1=ALU.subtract).then_inc(h0_ready, 1)

            def incidence(b, q):
                dve.wait_ge(adj_loaded[q], b.count(16, 16))
                if q == 0:
                    wait_reuse(dve, e_done, b.count(T, -T))
                for ct in range(QT * q, QT * (q + 1)):
                    V.tensor_scalar(inc[:, b.slot, ct, :], adj_in[:, ct, :], 0.0, None,
                                    ALU.not_equal).then_inc(inc_ready, 1)

            def degree(b, ct):
                if ct == 0:
                    dve.wait_ge(w_loaded, b.count(16, 16))
                if ct % QT == 0:
                    dve.wait_ge(adj_loaded[ct // QT], b.count(16, 16))
                wait_reuse(dve, deg_done, b.count(T, ct))
                V.scalar_tensor_tensor(out=junk[:, :], in0=adj_in[:, ct, :], scalar=0.0, in1=edge_w[:, :],
                                       op0=ALU.not_equal, op1=ALU.mult,
                                       accum_out=deg[:, ct:ct + 1]).then_inc(deg_done, 1)

            def node_inverse(b):
                dve.wait_ge(deg_done, b.count(T, T))
                V.tensor_scalar(dn_tmp[:, 0, :], deg[:, :], LEAST, None, ALU.max).then_inc(dn_step, 1)
                dve.wait_ge(dn_step, b.count(N_STEPS, 1))
                V.reciprocal(dn_tmp[:, 1, :], dn_tmp[:, 0, :]).then_inc(dn_step, 1)
                dve.wait_ge(dn_step, b.count(N_STEPS, 2))
                V.scalar_tensor_tensor(out=dn_tmp[:, 2, :], in0=deg[:, :], scalar=0.0, in1=dn_tmp[:, 1, :],
                                       op0=ALU.is_gt, op1=ALU.mult).then_inc(dn_step, 1)
                dve.wait_ge(dn_step, b.count(N_STEPS, 3))
                V.tensor_scalar(dn1[:, b.slot, :], dn_tmp[:, 2, :], wr[:, 4:5], None, ALU.mult).then_inc(dn_step, 1)
                V.tensor_scalar(dn2[:, b.slot, :], dn_tmp[:, 2, :], wr[:, 5:6], None, ALU.mult).then_inc(dn_step, 1)

            def b_lo(b, j):
                dve.wait_ge(pt_hi, b.count(4, j + 1))
                dt, half = j % 2, j // 2
                cols = slice(BANK * half, BANK * (half + 1))
                V.scalar_tensor_tensor(out=pt[:, dt, LO, cols], in0=wide[j][:, :], scalar=PT_SCALE,
                                       in1=pt[:, dt, HI, cols], op0=ALU.mult, op1=ALU.subtract).then_inc(pt_ready, 1)

            def phase_b(b, bx):
                if bx is not None:
                    x_stats(bx)
                b_lo(b, 0)
                if bx is not None:
                    inverse_root(x_ln, x_step, bx, X_STEPS, 1.0)
                    h0_lo(bx, 0)
                b_lo(b, 1)
                if bx is not None:
                    h0_lo(bx, 1)
                    h0_lo(bx, 2)
                b_lo(b, 2)
                if bx is not None:
                    h0_lo(bx, 3)
                b_lo(b, 3)

            def phase_c(b):
                if isinstance(b.loop, int) and b.offset == 0:
                    dve.wait_ge(rows_loaded, 32)
                for t in range(T + 1):
                    if t < T:
                        dve.wait_ge(c_done, b.count(T, t + 1))
                        if t == 0:
                            dve.wait_ge(dn_step, b.count(N_STEPS, N_STEPS))
                            wait_reuse(dve, d_done, b.count(T, 0))
                        V.scalar_tensor_tensor(out=z[:, t, :], in0=wide[t % 4][:, :], scalar=dn1[:, b.slot, t:t + 1],
                                               in1=b1_row[:, :], op0=ALU.mult, op1=ALU.add).then_inc(c_drained, 1)
                    if t >= 1:
                        dve.wait_ge(z_relu, b.count(T, t))
                        V.bn_stats(stat[:, t - 1, :], z[:, t - 1, :]).then_inc(z_stat, 1)
                variance(z_ln, z_stat, z_step, b, Z_STEPS, DH)

            def z_lo(b, t):
                dve.wait_ge(zs_hi, b.count(T, t + 1))
                V.tensor_tensor(zs[:, t % ZRING, LO, :], z[:, t, :], zs[:, t % ZRING, HI, :],
                                ALU.subtract).then_inc(zs_ready, 1)

            def phase_d(b):
                def add_bias(t):
                    dve.wait_ge(d_done, b.count(T, t + 1))
                    if t >= 2:
                        dve.wait_ge(xw_ready, b.count(T, t - 1))
                    V.scalar_tensor_tensor(out=xf[:, t % 2, :], in0=narrow[t % 4][:, 0:DOUT], scalar=XW_SCALE,
                                           in1=bw_row[:, :], op0=ALU.mult, op1=ALU.add).then_inc(xf_ready, 1)

                def xw_lo(t):
                    dve.wait_ge(xw_hi, b.count(T, t + 1))
                    V.tensor_tensor(xw[:, t, LO, :], xf[:, t % 2, :], xw[:, t, HI, :],
                                    ALU.subtract).then_inc(xw_ready, 1)

                for t in range(T):
                    add_bias(t)
                    if t >= 1:
                        xw_lo(t - 1)
                xw_lo(T - 1)

            def phase_e(b, bd):
                for et in range(T):
                    dve.wait_ge(t2_hi, b.count(T, et + 1))
                    V.scalar_tensor_tensor(out=edge[:, et, LO, :], in0=narrow[et % 4][:, 0:DOUT],
                                           scalar=be[:, b.slot, et:et + 1], in1=edge[:, et, HI, :],
                                           op0=ALU.mult, op1=ALU.subtract).then_inc(t2_ready, 1)
                    if bd is not None:
                        degree(bd, et)

            def phase_f(b, bi, bz):
                if bz is not None:
                    inverse_root(z_ln, z_step, bz, Z_STEPS, ZN_SCALE)
                for ct in range(T):
                    if bi is not None and ct < QUARTERS:
                        incidence(bi, ct)
                    if b is not None:
                        dve.wait_ge(f_done, b.count(T, ct + 1))
                        if ct == 0:
                            dve.wait_ge(res_ready, b.count(1, 1))
                        V.scalar_tensor_tensor(out=res[:, b.slot, ct, :], in0=narrow[ct % 4][:, 0:DOUT],
                                               scalar=dn2[:, b.slot, ct:ct + 1], in1=res[:, b.slot, ct, :],
                                               op0=ALU.mult, op1=ALU.add).then_inc(out_ready, 1)
                    if bz is not None:
                        z_lo(bz, ct)

            def bank_of_a(b, et):
                return (narrow + wide)[et] if isinstance(b.loop, int) and b.offset == 0 else narrow[et % 4]

            def edge_inverse(b, et):
                dve.wait_ge(a_done, b.count(T, et + 1))
                V.tensor_scalar(be_cnt[:, et:et + 1], bank_of_a(b, et)[:, ONE:ONE + 1], 1.0, None,
                                ALU.max).then_inc(be_step, 1)
                dve.wait_ge(be_step, b.count(2 * T, 2 * et + 1))
                V.reciprocal(be[:, b.slot, et:et + 1], be_cnt[:, et:et + 1]).then_inc(be_step, 1)

            def t1_lo_part(b, et):
                dve.wait_ge(t1_hi, b.count(T, et + 1))
                V.scalar_tensor_tensor(out=edge[:, et, LO, :], in0=bank_of_a(b, et)[:, 0:DIN],
                                       scalar=be[:, b.slot, et:et + 1], in1=edge[:, et, HI, :],
                                       op0=ALU.mult, op1=ALU.subtract).then_inc(t1_ready, 1)

            def phase_a(b):
                for et in range(T):
                    edge_inverse(b, et)
                    t1_lo_part(b, et)

            def extremes(src, rest, i):
                for sign in range(2):
                    if i + sign > 0:
                        dve.wait_ge(max_step, 2 * i + sign)
                    V.tensor_scalar(rest, src, 1.0 - 2.0 * sign, None, ALU.mult, ALU.max,
                                    accum_out=wext[:, i, sign:sign + 1]).then_inc(max_step, 1)

            b0 = Batch(0, 0)
            x_stats(b0)
            dve.wait_ge(weights_loaded, 64)
            for ht in range(HT_):
                last = V.tensor_copy(beta_cols[:, ht, :], gb[:, 1, ht:ht + 1].to_broadcast([P, P]))
            last.then_inc(beta_ready, 1)
            inverse_root(x_ln, x_step, b0, X_STEPS, 1.0)
            incidence(b0, 0)
            dve.wait_ge(bias_done, 1)
            V.tensor_copy(bw_row[:, :], narrow[3][:, 0:DOUT]).then_inc(bias_read, 1)
            h0_lo(b0, 0)
            for ht in range(HT_):
                last = V.tensor_scalar(gf[:, ht, :], w2f[:, ht, :], gb[:, 0, ht:ht + 1], None, ALU.mult)
            last.then_inc(setup_step, 1)
            h0_lo(b0, 1)
            incidence(b0, 1)
            extremes(w1f, junk[:, :], 0)
            h0_lo(b0, 2)
            incidence(b0, 2)
            dve.wait_ge(setup_step, 1)
            extremes(gf, junk[:, :], 1)
            h0_lo(b0, 3)
            incidence(b0, 3)
            dve.wait_ge(bias_read, 1)
            extremes(bw_row[:, :], junk[:, 0:DOUT], 2)
            dve.wait_ge(max_step, 6)
            V.tensor_reduce(wm[:, 0:3], wext[:, :, :], mybir.AxisListType.X, ALU.max).then_inc(setup_step, 1)
            dve.wait_ge(setup_step, 2)
            V.scalar_tensor_tensor(out=wm[:, 1:2], in0=wm[:, 2:3], scalar=BIAS_ROOM, in1=wm[:, 1:2],
                                   op0=ALU.mult, op1=ALU.max).then_inc(max_here, 1)
            dve.wait_ge(max_all, 1)
            V.tensor_scalar(wall[:, :], wall[:, :], TINY, None, ALU.max).then_inc(setup_step, 1)
            dve.wait_ge(setup_step, 3)
            V.tensor_scalar(wp[:, :].bitcast(U32), wall[:, :].bitcast(U32), EXPONENT, None,
                            ALU.bitwise_and).then_inc(setup_step, 1)
            dve.wait_ge(setup_step, 4)
            V.reciprocal(wr[:, 0:2], wp[:, :])
            V.tensor_scalar(wr[:, 4:5], wp[:, 0:1], 1.0 / (H0_SCALE * PT_SCALE * W_SCALE), None, ALU.mult)
            V.tensor_scalar(wr[:, 5:6], wp[:, 1:2], 1.0 / (ZN_SCALE * W_SCALE * XW_SCALE), None,
                            ALU.mult).then_inc(setup_step, 1)
            dve.wait_ge(setup_step, 5)
            V.tensor_scalar(w1f, w1f, wr[:, 0:1], W_SCALE, ALU.mult, ALU.mult).then_inc(setup_step, 1)
            V.tensor_scalar(gf, gf, wr[:, 1:2], W_SCALE, ALU.mult, ALU.mult).then_inc(setup_step, 1)
            V.tensor_scalar(bw_row[:, :], bw_row[:, :], wr[:, 1:2], ZN_SCALE * W_SCALE * XW_SCALE,
                            ALU.mult, ALU.mult).then_inc(setup_step, 1)
            dve.wait_ge(w_hi, 1)
            V.tensor_tensor(w1s[:, :, LO, :], w1f, w1s[:, :, HI, :], ALU.subtract).then_inc(w_ready, 1)
            dve.wait_ge(w_hi, 2)
            V.tensor_tensor(w2s[:, :, LO, :], gf, w2s[:, :, HI, :], ALU.subtract).then_inc(w_ready, 1)
            for et in range(T):
                edge_inverse(b0, et)
            for et in range(T):
                t1_lo_part(b0, et)
            for ct in range(T):
                degree(b0, ct)
            node_inverse(b0)
            phase_b(b0, Batch(0, 1))
            phase_c(b0)
            for q in range(QUARTERS):
                incidence(Batch(0, 1), q)
            inverse_root(z_ln, z_step, b0, Z_STEPS, ZN_SCALE)
            for t in range(T):
                edge_inverse(Batch(0, 1), t)
                z_lo(b0, t)
                degree(Batch(0, 1), t)
                t1_lo_part(Batch(0, 1), t)
            node_inverse(Batch(0, 1))
            with dve.Fori(0, N - 2, 2) as n:
                for k in range(2):
                    phase_d(Batch(n, k))
                    phase_b(Batch(n, k + 1), Batch(n, k + 2))
                    phase_e(Batch(n, k), Batch(n, k + 2))
                    phase_c(Batch(n, k + 1))
                    phase_f(Batch(n, k), Batch(n, k + 2), Batch(n, k + 1))
                    phase_a(Batch(n, k + 2))
                    node_inverse(Batch(n, k + 2))
            phase_d(Batch(0, N - 2))
            phase_b(Batch(0, N - 1), None)
            phase_e(Batch(0, N - 2), None)
            phase_c(Batch(0, N - 1))
            phase_f(Batch(0, N - 2), None, Batch(0, N - 1))
            phase_d(Batch(0, N - 1))
            phase_e(Batch(0, N - 1), None)
            phase_f(Batch(0, N - 1), None, None)
    return nc


def kernel(x, adj, L0_gnn_W1, L0_gnn_b1, L0_gnn_gamma, L0_gnn_beta, L0_gnn_W2, L0_gnn_b2):
    import numpy as np
    import concourse.bacc as bacc
    from concourse.bass_utils import run_bass_kernel_spmd as run

    arrays = {
        "x": np.ascontiguousarray(x),
        "adj": np.ascontiguousarray(adj),
        "w1t": np.ascontiguousarray(np.transpose(L0_gnn_W1)),
        "b1": np.ascontiguousarray(np.reshape(L0_gnn_b1, (1, -1))),
        "gamma": np.ascontiguousarray(np.transpose(np.reshape(L0_gnn_gamma, (-1, P)))),
        "beta": np.ascontiguousarray(np.transpose(np.reshape(L0_gnn_beta, (-1, P)))),
        "w2t": np.ascontiguousarray(np.transpose(L0_gnn_W2)),
        "b2": np.ascontiguousarray(np.reshape(L0_gnn_b2, (1, -1))),
    }
    nc = bacc.Bacc("TRN2", target_bir_lowering=False, num_devices=1)
    ins = [nc.dram_tensor(name, a.shape, mybir.dt.from_np(a.dtype), kind="ExternalInput").ap()
           for name, a in arrays.items()]
    out = nc.dram_tensor("out", arrays["x"].shape, F32, kind="ExternalOutput").ap()
    hypergraph_block(nc, *ins, out)
    return run(nc, [arrays], core_ids=[0]).results[0]["out"]
```

```python
from contextlib import ExitStack

import concourse.bass as bass
from concourse import mybir

ALU = mybir.AluOpType
ACT = mybir.ActivationFunctionType
RMAX = bass.bass_isa.ReduceOp.max
F32 = mybir.dt.float32
F16 = mybir.dt.float16
BF16 = mybir.dt.bfloat16
U32 = mybir.dt.uint32

P = 128
BANK = 512
HI, LO = 0, 1

H0_SCALE = 2.0 ** 8
PT_SCALE = 2.0 ** -7
W_SCALE = 2.0 ** 8
ZN_SCALE = 2.0 ** 4
XW_SCALE = 2.0 ** -7
BIAS_ROOM = 2.0 ** -8
TINY = 2.0 ** -100
LEAST = 2.0 ** -126
EXPONENT = 0x7F800000
EPS = 1e-5


class Batch:

    def __init__(self, loop, offset):
        self.loop, self.offset, self.slot = loop, offset, offset % 2

    def next(self, k):
        return Batch(self.loop, self.offset + k)

    def index(self):
        return self.loop + self.offset

    def count(self, per_batch, more):
        return self.loop * per_batch + (self.offset * per_batch + more)


def wait_reuse(eng, sem, value):
    if not (isinstance(value, int) and value <= 0):
        eng.wait_ge(sem, value)


def hypergraph_block(nc, x, adj, w1t, b1, gamma, beta, w2t, b2, out):
    N, C, DIN = x.shape
    DH = w1t.shape[1]
    DOUT = w2t.shape[1]
    T = C // P
    DT = DIN // P
    HT_ = DH // P
    assert C == 1024 and T == 8 and DIN == DOUT == 256 and DH == BANK and N % 2 == 0 and N >= 4
    ONE = DIN
    LO_AT = DIN + 8
    HL = LO_AT + DIN
    GROUPS = 4
    GT = T // GROUPS
    QUARTERS = 4
    QT = T // QUARTERS
    X_STEPS, Z_STEPS, N_STEPS = 11, 11, 5
    EARLY_DEGREES = (3, 5)
    Z_BEHIND = 2
    ZRING = 6

    with ExitStack() as ctx:
        def sb(name, shape, dt=F32):
            return ctx.enter_context(nc.sbuf_tensor(name, shape, dt))

        def sem(name):
            return ctx.enter_context(nc.semaphore(name))

        adj_in = sb("adj_in", [P, T, C])
        inc = sb("incidence", [P, 2, T, C], BF16)
        inc_t = sb("incidence_t", [P, 2, T, T, P], BF16)
        x_in = sb("x_in", [P, T, DIN])
        u = sb("h0_ring", [P, 2, GT, DIN])
        h0 = sb("h0_split", [P, T, HL], F16)
        res = sb("residual", [P, 2, T, DOUT])
        edge = sb("edge_means", [P, T, 2, DIN], F16)
        pt = sb("pt_split", [P, DT, 2, C], F16)
        z = sb("z", [P, T, DH])
        zt = z[:, :, :].bitcast(F16).rearrange("p t (k c) -> p t k c", c=P)
        zs = sb("z_split_ring", [P, ZRING, 2, DH], F16)
        xw = sb("xw_split", [P, T, 2, DOUT], F16)
        xf = sb("xw_ring", [P, 2, DOUT])
        w1s = sb("w1_split", [P, DT, 2, DH], F16)
        w2s = sb("w2_split", [P, HT_, 2, DOUT], F16)
        b1_row = sb("b1_row", [P, DH])
        b2_row = sb("b2_row", [P, DOUT])
        bw_row = sb("bias_w2_row", [P, DOUT])
        edge_w = sb("edge_weights", [P, C])
        junk = sb("junk", [P, C])
        stat = sb("stat", [P, T, 6])
        x_ln = sb("x_ln", [P, 7, T])
        z_ln = sb("z_ln", [P, 7, T])
        deg = sb("node_degree", [P, T])
        dn_tmp = sb("dn_tmp", [P, 3, T])
        dn1 = sb("dn_conv1", [P, 2, T])
        dn2 = sb("dn_conv2", [P, 2, T])
        be_cnt = sb("edge_count", [P, T])
        be = sb("edge_inverse", [P, 2, T])
        gb = sb("gamma_beta", [P, 2, HT_])
        wm = sb("weight_max", [P, 4])
        wall = sb("weight_max_all", [P, 2])
        wp = sb("weight_power", [P, 2])
        wr = sb("weight_factor", [P, 6])
        w1f = z[:, 0:2, :]
        w2f = z[:, 2:4, :].rearrange("p a (b o) -> p (a b) o", o=DOUT)
        gf = z[:, 4:6, :].rearrange("p a (b o) -> p (a b) o", o=DOUT)
        beta_cols = z[:, 6, :].rearrange("p (t m) -> p t m", m=P)

        narrow = [ctx.enter_context(nc.psum_tensor(f"narrow{i}", [P, BANK], F32)) for i in range(4)]
        wide = [ctx.enter_context(nc.psum_tensor(f"wide{i}", [P, BANK], F32)) for i in range(4)]
        first_banks = wide + narrow

        x_loaded = sem("x_loaded")
        w_loaded = sem("w_loaded")
        adj_loaded = [sem(f"adj_loaded{q}") for q in range(QUARTERS)]
        x_first = sem("x_first")
        weights_loaded = sem("weights_loaded")
        w1_loaded = sem("w1_loaded")
        rows_loaded = sem("rows_loaded")
        stored = [sem(f"stored{q}") for q in range(QUARTERS)]
        ones_set = sem("ones_set")
        max_here = sem("max_here")
        max_all = sem("max_all")
        setup_step = sem("setup_step")
        beta_ready = sem("beta_ready")
        gamma_w2 = sem("gamma_w2")
        bias_done = sem("bias_done")
        bias_read = sem("bias_read")
        w_hi = sem("w_hi")
        w_ready = sem("w_ready")
        x_stat = sem("x_stat")
        x_step = sem("x_step")
        u_ready = sem("u_ready")
        h0_hi = sem("h0_hi")
        h0_ready = sem("h0_ready")
        x_added = sem("x_added")
        res_ready = sem("res_ready")
        inc_ready = sem("inc_ready")
        deg_done = sem("deg_done")
        dn_step = sem("dn_step")
        a_done = sem("a_done")
        be_step = sem("be_step")
        t1_hi = sem("t1_hi")
        t1_ready = sem("t1_ready")
        inc_t_ready = [sem(f"inc_t_ready{q}") for q in range(QUARTERS)]
        b_done = sem("b_done")
        pt_hi = sem("pt_hi")
        pt_ready = sem("pt_ready")
        c_done = sem("c_done")
        c_drained = sem("c_drained")
        z_relu = sem("z_relu")
        z_stat = sem("z_stat")
        z_step = sem("z_step")
        zs_hi = sem("zs_hi")
        zs_ready = sem("zs_ready")
        zt_ready = [sem(f"zt_ready{q}") for q in range(QUARTERS)]
        d_done = sem("d_done")
        xf_ready = sem("xf_ready")
        xw_hi = sem("xw_hi")
        xw_ready = sem("xw_ready")
        e_done = sem("e_done")
        t2_hi = sem("t2_hi")
        t2_ready = sem("t2_ready")
        f_done = sem("f_done")
        out_ready = sem("out_ready")

        def rows(ap, b):
            if isinstance(b.loop, int):
                part = ap[b.offset:b.offset + 1]
            else:
                part = ap[bass.ds(b.index(), 1)]
            return part.rearrange("b (p t) d -> p (b t) d", t=T)

        block = ctx.enter_context(nc.Block())

        @block.sync
        def _(sp):
            def load_x(b):
                wait_reuse(sp, res_ready, b.count(1, 0))
                sp.dma_start(x_in[:, :, :], rows(x, b)).then_inc(x_loaded, 16)

            def load_adj(b, q):
                wait_reuse(sp, inc_ready, b.count(T, QT * (q + 1) - T))
                sp.dma_start(adj_in[:, QT * q:QT * (q + 1), :],
                             rows(adj, b)[:, QT * q:QT * (q + 1), :]).then_inc(adj_loaded[q], 16)

            def load_edge_weights(b):
                wait_reuse(sp, deg_done, b.count(T, 0))
                if isinstance(b.loop, int):
                    first = adj[b.offset:b.offset + 1, 0, :]
                else:
                    first = adj[bass.ds(b.index(), 1), 0, :]
                sp.dma_start(edge_w[:, :], first.to_broadcast([P, C])).then_inc(w_loaded, 16)

            def transpose_inc(b, q):
                ts = slice(QT * q, QT * (q + 1))
                sp.dma_start_transpose(inc_t[:, b.slot, ts, :, :].rearrange("p a k c -> p (a k) c"),
                                       inc[:, b.slot, ts, :].rearrange("p a e -> p (a e)"))\
                    .then_inc(inc_t_ready[q], 16)

            def transpose_z(b, q):
                slot = QT * q % ZRING
                sp.dma_start_transpose(zt[:, QT * q:QT * (q + 1), :, :].rearrange("p a k c -> p (a k) c"),
                                       zs[:, slot:slot + QT, :, :].rearrange("p a b h -> p (a b h)"))\
                    .then_inc(zt_ready[q], 16)

            def store(b, q):
                ts = slice(QT * q, QT * (q + 1))
                sp.dma_start(rows(out, b)[:, ts, :], res[:, b.slot, ts, :]).then_inc(stored[q], 16)

            def step(b, load=True, turn_h=True, turn_z=True):
                for q in range(QUARTERS):
                    if turn_z:
                        sp.wait_ge(zs_ready, b.count(T, T + QT * (q + 1)))
                    if turn_h and q == QUARTERS - 1:
                        sp.wait_ge(inc_ready, b.count(QUARTERS, 3 * QUARTERS) * QT)
                    sp.wait_ge(out_ready, b.count(QUARTERS, q + 1) * QT)
                    store(b, q)
                    if turn_z:
                        transpose_z(b.next(1), q)
                if turn_h:
                    for q in range(QUARTERS):
                        transpose_inc(b.next(2), q)
                    load_edge_weights(b.next(2))
                if load:
                    load_x(b.next(3))
                    for q in range(QUARTERS):
                        load_adj(b.next(3), q)

            x_rows = rows(x, Batch(0, 0))
            sp.dma_start(x_in[:, 0:T // 2, :], x_rows[:, 0:T // 2, :]).then_inc(x_first, 16)
            sp.dma_start(x_in[:, T // 2:T, :], x_rows[:, T // 2:T, :]).then_inc(x_loaded, 16)
            sp.dma_start(gb[:, 1, :], beta).then_inc(weights_loaded, 16)
            sp.dma_start(gb[:, 0, :], gamma).then_inc(weights_loaded, 16)
            sp.dma_start(w2f, w2t.rearrange("(t p) o -> p t o", p=P)).then_inc(weights_loaded, 16)
            load_adj(Batch(0, 0), 0)
            sp.dma_start(w1f, w1t.rearrange("(t p) h -> p t h", p=P)).then_inc(w1_loaded, 16)
            sp.dma_start(b2_row[:, :], b2.to_broadcast([P, DOUT])).then_inc(rows_loaded, 16)
            for q in range(1, QUARTERS):
                load_adj(Batch(0, 0), q)
            load_edge_weights(Batch(0, 0))
            sp.dma_start(b1_row[:, :], b1.to_broadcast([P, DH])).then_inc(rows_loaded, 16)
            for q in range(QUARTERS):
                sp.wait_ge(inc_ready, QT * (q + 1))
                transpose_inc(Batch(0, 0), q)
            load_x(Batch(0, 1))
            for q in range(QUARTERS):
                load_adj(Batch(0, 1), q)
            load_edge_weights(Batch(0, 1))
            for q in range(QUARTERS):
                sp.wait_ge(inc_ready, T + QT * (q + 1))
                transpose_inc(Batch(0, 1), q)
            load_x(Batch(0, 2))
            for q in range(QUARTERS):
                load_adj(Batch(0, 2), q)
            for q in range(QUARTERS):
                sp.wait_ge(zs_ready, QT * (q + 1))
                transpose_z(Batch(0, 0), q)
            with sp.Fori(0, N - 5, 2) as n:
                for k in range(2):
                    step(Batch(n, k))
            step(Batch(0, N - 4))
            step(Batch(0, N - 3), load=False)
            step(Batch(0, N - 2), load=False, turn_h=False)
            step(Batch(0, N - 1), load=False, turn_h=False, turn_z=False)
            for q in range(QUARTERS):
                sp.wait_ge(stored[q], 16 * N)

        @block.gpsimd
        def _(pool):
            nc.gpsimd.memset(h0[:, :, ONE:ONE + 1], 1.0).then_inc(ones_set, 1)

            def residual(b):
                for g in range(GROUPS):
                    pool.wait_ge(u_ready, b.count(T, GT * (g + 1)))
                    xs = x_in[:, GT * g:GT * (g + 1), :]
                    nc.gpsimd.tensor_tensor(xs, xs, u[:, g % 2, :, :], ALU.add).then_inc(x_added, 1)
                pool.wait_ge(x_added, b.count(GROUPS, GROUPS))
                if isinstance(b.loop, int) and b.offset == 0:
                    pool.wait_ge(rows_loaded, 32)
                for q in range(QUARTERS):
                    wait_reuse(pool, stored[q], b.count(16, -16))
                nc.gpsimd.tensor_tensor(res[:, b.slot, :, :], x_in[:, :, :],
                                        b2_row[:, None, :].to_broadcast([P, T, DOUT]),
                                        ALU.add).then_inc(res_ready, 1)

            residual(Batch(0, 0))
            pool.wait_ge(max_here, 1)
            nc.gpsimd.partition_all_reduce(wall[:, :], wm[:, 0:2], P, RMAX).then_inc(max_all, 1)
            pool.wait_ge(w_hi, 1)
            nc.gpsimd.tensor_tensor(w1s[:, :, LO, :], w1f, w1s[:, :, HI, :], ALU.subtract).then_inc(w_ready, 1)
            pool.wait_ge(w_hi, 2)
            nc.gpsimd.tensor_tensor(w2s[:, :, LO, :], gf, w2s[:, :, HI, :], ALU.subtract).then_inc(w_ready, 1)
            residual(Batch(0, 1))
            with pool.Fori(0, N - 2, 2) as n:
                for k in range(2):
                    residual(Batch(n, k + 2))

        @block.tensor
        def _(pe):
            def take_narrow(b, t, own, before, b_before):
                if t >= 4:
                    pe.wait_ge(own, b.count(T, t - 3))
                elif b_before is not None:
                    pe.wait_ge(before, b_before.count(T, t + 5))
                return narrow[t % 4]

            def first_stage_a():
                b = Batch(0, 0)
                half = T // 2
                order = [(ct, et) for ct in range(half) for et in range(T)]
                order += [(ct, et) for et in range(T) for ct in range(half, T)]
                pe.wait_ge(ones_set, 1)
                for ct, et in order:
                    if et == 0:
                        pe.wait_ge(inc_ready, ct + 1)
                        pe.wait_ge(h0_ready, ct // GT + 1)
                    acc = first_banks[et]
                    if ct == 0 and acc is narrow[3]:
                        pe.wait_ge(bias_read, 1)
                    cols = slice(P * et, P * (et + 1))
                    nc.tensor.matmul(acc[:, 0:ONE + 1], inc[:, b.slot, ct, cols], h0[:, ct, 0:ONE + 1],
                                     start=(ct == 0), stop=False)
                    last = nc.tensor.matmul(acc[:, 0:DIN], inc[:, b.slot, ct, cols], h0[:, ct, LO_AT:HL],
                                            start=False, stop=(ct == T - 1))
                    if ct == T - 1:
                        last.then_inc(a_done, 1)

            def stage_a(b):
                opening = isinstance(b.loop, int) and b.offset < 2
                pe.wait_ge(inc_ready, b.count(T, T))
                pe.wait_ge(h0_ready, b.count(GROUPS, GROUPS))
                for et in range(T):
                    if opening:
                        acc = take_narrow(b, et, t1_ready, t1_ready, None)
                    else:
                        acc = take_narrow(b, et, t1_ready, out_ready, b.next(-2))
                    cols = slice(P * et, P * (et + 1))
                    for ct in range(T):
                        nc.tensor.matmul(acc[:, 0:ONE + 1], inc[:, b.slot, ct, cols], h0[:, ct, 0:ONE + 1],
                                         start=(ct == 0), stop=False)
                        last = nc.tensor.matmul(acc[:, 0:DIN], inc[:, b.slot, ct, cols], h0[:, ct, LO_AT:HL],
                                                start=False, stop=(ct == T - 1))
                    last.then_inc(a_done, 1)

            def stage_b(b):
                for j in range(4):
                    dt, half = j % 2, j // 2
                    if dt == 0:
                        for q in (2 * half, 2 * half + 1):
                            pe.wait_ge(inc_t_ready[q], b.count(16, 16))
                    if not (isinstance(b.loop, int) and b.offset == 0):
                        pe.wait_ge(c_drained, b.count(T, 5 + j - T))
                    for et in range(T):
                        if j == 0:
                            pe.wait_ge(t1_ready, b.count(T, et + 1))
                        for part in (HI, LO):
                            last = nc.tensor.matmul(wide[j][:, :], edge[:, et, part, P * dt:P * (dt + 1)],
                                                    inc_t[:, b.slot, 4 * half:4 * (half + 1), et, :],
                                                    start=(et == 0 and part == HI), stop=(et == T - 1 and part == LO))
                    last.then_inc(b_done, 1)

            def stage_c(b):
                if isinstance(b.loop, int) and b.offset == 0:
                    pe.wait_ge(w_ready, 1)
                for t in range(T):
                    pe.wait_ge(pt_ready, b.count(4, max(2 * (t // 4 + 1), min(t + 1, 4))))
                    if t >= 4:
                        pe.wait_ge(c_drained, b.count(T, t - 3))
                    k = 0
                    for dt in range(DT):
                        for left, right in ((HI, HI), (HI, LO), (LO, HI)):
                            last = nc.tensor.matmul(wide[t % 4][:, :], pt[:, dt, left, P * t:P * (t + 1)],
                                                    w1s[:, dt, right, :], start=(k == 0), stop=(k == 3 * DT - 1))
                            k += 1
                    last.then_inc(c_done, 1)

            def stage_d(b):
                final = isinstance(b.loop, int) and b.offset == N - 1
                if isinstance(b.loop, int) and b.offset == 0:
                    pe.wait_ge(w_ready, 2)
                for t in range(T):
                    if final:
                        acc = take_narrow(b, t, xf_ready, out_ready, b.next(-1))
                    else:
                        acc = take_narrow(b, t, xf_ready, t1_ready, b.next(1))
                    if t % QT == 0:
                        pe.wait_ge(zt_ready[t // QT], b.count(16, 16))
                    k = 0
                    for ht in range(HT_):
                        for left, right in ((HI, HI), (HI, LO), (LO, HI)):
                            last = nc.tensor.matmul(acc[:, 0:DOUT], zt[:, t, HT_ * left + ht, :],
                                                    w2s[:, ht, right, :], start=(k == 0), stop=(k == 3 * HT_ - 1))
                            k += 1
                    last.then_inc(d_done, 1)

            def stage_e(b):
                for et in range(T):
                    acc = take_narrow(b, et, t2_ready, xf_ready, b)
                    for ct in range(T):
                        if et == 0:
                            pe.wait_ge(xw_ready, b.count(T, ct + 1))
                        for part in (HI, LO):
                            last = nc.tensor.matmul(acc[:, 0:DOUT], inc[:, b.slot, ct, P * et:P * (et + 1)],
                                                    xw[:, ct, part, :],
                                                    start=(ct == 0 and part == HI), stop=(ct == T - 1 and part == LO))
                    last.then_inc(e_done, 1)

            def stage_f(b):
                for ct in range(T):
                    acc = take_narrow(b, ct, out_ready, t2_ready, b)
                    for et in range(T):
                        if ct == 0:
                            pe.wait_ge(t2_ready, b.count(T, et + 1))
                        for part in (HI, LO):
                            last = nc.tensor.matmul(acc[:, 0:DOUT], inc_t[:, b.slot, ct, et, :],
                                                    edge[:, et, part, :],
                                                    start=(et == 0 and part == HI), stop=(et == T - 1 and part == LO))
                    last.then_inc(f_done, 1)

            pe.wait_ge(beta_ready, 1)
            for ht in range(HT_):
                last = nc.tensor.matmul(narrow[3][:, 0:DOUT], beta_cols[:, ht, :], w2f[:, ht, :],
                                        start=(ht == 0), stop=(ht == HT_ - 1))
            last.then_inc(bias_done, 1)
            first_stage_a()
            stage_b(Batch(0, 0))
            stage_c(Batch(0, 0))
            stage_a(Batch(0, 1))
            with pe.Fori(0, N - 2, 2) as n:
                for k in range(2):
                    stage_d(Batch(n, k))
                    stage_b(Batch(n, k + 1))
                    stage_e(Batch(n, k))
                    stage_c(Batch(n, k + 1))
                    stage_f(Batch(n, k))
                    stage_a(Batch(n, k + 2))
            stage_d(Batch(0, N - 2))
            stage_b(Batch(0, N - 1))
            stage_e(Batch(0, N - 2))
            stage_c(Batch(0, N - 1))
            stage_f(Batch(0, N - 2))
            stage_d(Batch(0, N - 1))
            stage_e(Batch(0, N - 1))
            stage_f(Batch(0, N - 1))

        @block.scalar
        def _(act):
            def copy(o, i, **kw):
                return nc.scalar.activation(o, i, ACT.Copy, **kw)

            def root_x(b):
                act.wait_ge(x_step, b.count(X_STEPS, 4))
                nc.scalar.activation(x_ln[:, 1, :], x_ln[:, 0, :], ACT.Sqrt).then_inc(x_step, 1)

            def h0_tiles(b, g):
                if g == 0:
                    act.wait_ge(x_step, b.count(X_STEPS, X_STEPS))
                wait_reuse(act, x_added, b.count(GROUPS, g - 1))
                wait_reuse(act, h0_ready, b.count(GROUPS, g - 1))
                for i in range(GT):
                    t = GT * g + i
                    nc.scalar.activation(u[:, g % 2, i, :], x_in[:, t, :], ACT.Relu, scale=x_ln[:, 4, t:t + 1],
                                         bias=x_ln[:, 6, t:t + 1]).then_inc(u_ready, 1)

            def h0_hi_part(b, g):
                act.wait_ge(u_ready, b.count(T, GT * (g + 1)))
                if g == 0:
                    wait_reuse(act, a_done, b.count(T, 0))
                copy(h0[:, GT * g:GT * (g + 1), 0:DIN], u[:, g % 2, :, :], scale=H0_SCALE).then_inc(h0_hi, 1)

            def z_split(b, t):
                if t == 0:
                    act.wait_ge(z_step, b.count(Z_STEPS, Z_STEPS))
                if t % QT == 0:
                    if t >= ZRING:
                        act.wait_ge(zt_ready[(t - ZRING) // QT], b.count(16, 16))
                    else:
                        wait_reuse(act, zt_ready[(t if t + ZRING >= T else t + ZRING) // QT], b.count(16, 0))
                by = dict(scale=z_ln[:, 4, t:t + 1], bias=z_ln[:, 6, t:t + 1])
                nc.scalar.activation(zs[:, t % ZRING, HI, :], z[:, t, :], ACT.Identity, **by)
                nc.scalar.activation(z[:, t, :], z[:, t, :], ACT.Identity, **by).then_inc(zs_hi, 1)

            def drain_b(b, j):
                act.wait_ge(b_done, b.count(4, j + 1))
                if j == 0:
                    wait_reuse(act, c_done, b.count(T, 0))
                dt, half = j % 2, j // 2
                copy(pt[:, dt, HI, BANK * half:BANK * (half + 1)], wide[j][:, :], scale=PT_SCALE).then_inc(pt_hi, 1)

            def phase_b(b, bx):
                drain_b(b, 0)
                if bx is not None:
                    root_x(bx)
                    h0_tiles(bx, 0)
                    h0_tiles(bx, 1)
                    h0_hi_part(bx, 0)
                drain_b(b, 1)
                if bx is not None:
                    h0_hi_part(bx, 1)
                    h0_tiles(bx, 2)
                    h0_tiles(bx, 3)
                    h0_hi_part(bx, 2)
                drain_b(b, 2)
                if bx is not None:
                    h0_hi_part(bx, 3)
                drain_b(b, 3)

            def z_relus(b):
                for t in range(T):
                    act.wait_ge(c_drained, b.count(T, t + 1))
                    nc.scalar.activation(z[:, t, :], z[:, t, :], ACT.Relu).then_inc(z_relu, 1)
                act.wait_ge(z_step, b.count(Z_STEPS, 4))
                nc.scalar.activation(z_ln[:, 1, :], z_ln[:, 0, :], ACT.Sqrt).then_inc(z_step, 1)

            def phase_c(b):
                z_relus(b)
                for t in range(T):
                    z_split(b, t)

            def phase_d(b):
                for t in range(T):
                    act.wait_ge(xf_ready, b.count(T, t + 1))
                    copy(xw[:, t, HI, :], xf[:, t % 2, :]).then_inc(xw_hi, 1)

            def phase_e(b):
                if isinstance(b.loop, int) and b.offset == N - 1:
                    act.wait_ge(f_done, b.count(T, 0))
                else:
                    act.wait_ge(b_done, b.count(4, 8))
                for et in range(T):
                    act.wait_ge(e_done, b.count(T, et + 1))
                    copy(edge[:, et, HI, :], narrow[et % 4][:, 0:DOUT], scale=be[:, b.slot, et:et + 1]).then_inc(t2_hi, 1)

            def t1_hi_part(b, et):
                act.wait_ge(be_step, b.count(2 * T, 2 * et + 2))
                bank = first_banks[et] if isinstance(b.loop, int) and b.offset == 0 else narrow[et % 4]
                copy(edge[:, et, HI, :], bank[:, 0:DIN], scale=be[:, b.slot, et:et + 1]).then_inc(t1_hi, 1)

            def phase_a(b):
                act.wait_ge(f_done, b.count(T, -T))
                for et in range(T):
                    t1_hi_part(b, et)

            act.wait_ge(ones_set, 1)
            nc.scalar.activation(wm[:, 3:4], h0[:, 0, ONE:ONE + 1], ACT.Sqrt)
            root_x(Batch(0, 0))
            for g in range(GROUPS):
                h0_tiles(Batch(0, 0), g)
                h0_hi_part(Batch(0, 0), g)
                if g == 0:
                    act.wait_ge(weights_loaded, 48)
                    for ht in range(HT_):
                        last = copy(gf[:, ht, :], w2f[:, ht, :], scale=gb[:, 0, ht:ht + 1])
                    last.then_inc(gamma_w2, 1)
            for et in range(T):
                t1_hi_part(Batch(0, 0), et)
            act.wait_ge(setup_step, 5)
            copy(w1s[:, :, HI, :], w1f, scale=wr[:, 2:3])
            copy(w1f, w1f, scale=wr[:, 2:3]).then_inc(w_hi, 1)
            copy(w2s[:, :, HI, :], gf, scale=wr[:, 3:4])
            copy(gf, gf, scale=wr[:, 3:4]).then_inc(w_hi, 1)
            phase_b(Batch(0, 0), Batch(0, 1))
            z_relus(Batch(0, 0))
            act.wait_ge(b_done, 4)
            for t in range(T):
                z_split(Batch(0, 0), t)
                t1_hi_part(Batch(0, 1), t)
            with act.Fori(0, N - 2, 2) as n:
                for k in range(2):
                    phase_d(Batch(n, k))
                    phase_b(Batch(n, k + 1), Batch(n, k + 2))
                    phase_e(Batch(n, k))
                    phase_c(Batch(n, k + 1))
                    phase_a(Batch(n, k + 2))
            phase_d(Batch(0, N - 2))
            phase_b(Batch(0, N - 1), None)
            phase_e(Batch(0, N - 2))
            phase_c(Batch(0, N - 1))
            phase_d(Batch(0, N - 1))
            phase_e(Batch(0, N - 1))

        @block.vector
        def _(dve):
            V = nc.vector

            def variance(ln, stat_sem, step_sem, b, steps, n):
                s, _, y, tmp, _, mean = (ln[:, i, :] for i in range(6))
                dve.wait_ge(stat_sem, b.count(T, T))
                V.tensor_tensor(mean, stat[:, :, 1], stat[:, :, 4], ALU.add)
                V.tensor_tensor(tmp, stat[:, :, 1], stat[:, :, 4], ALU.subtract)
                V.tensor_tensor(s, stat[:, :, 2], stat[:, :, 5], ALU.add).then_inc(step_sem, 1)
                dve.wait_ge(step_sem, b.count(steps, 1))
                V.tensor_scalar(mean, mean, 0.5, None, ALU.mult)
                V.tensor_tensor(y, tmp, tmp, ALU.mult).then_inc(step_sem, 1)
                dve.wait_ge(step_sem, b.count(steps, 2))
                V.scalar_tensor_tensor(out=tmp, in0=s, scalar=4.0 / n, in1=y, op0=ALU.mult,
                                       op1=ALU.add).then_inc(step_sem, 1)
                dve.wait_ge(step_sem, b.count(steps, 3))
                V.tensor_scalar(s, tmp, 0.25, EPS, ALU.mult, ALU.add).then_inc(step_sem, 1)

            def inverse_root(ln, step_sem, b, steps, scale):
                s, root, y, tmp, rstd = (ln[:, i, :] for i in range(5))
                dve.wait_ge(step_sem, b.count(steps, 5))
                V.reciprocal(y, root).then_inc(step_sem, 1)
                dve.wait_ge(step_sem, b.count(steps, 6))
                V.tensor_tensor(tmp, y, y, ALU.mult).then_inc(step_sem, 1)
                dve.wait_ge(step_sem, b.count(steps, 7))
                V.tensor_tensor(tmp, tmp, s, ALU.mult).then_inc(step_sem, 1)
                dve.wait_ge(step_sem, b.count(steps, 8))
                V.tensor_scalar(tmp, tmp, -0.5 * scale, 1.5 * scale, ALU.mult, ALU.add).then_inc(step_sem, 1)
                dve.wait_ge(step_sem, b.count(steps, 9))
                V.tensor_tensor(rstd, tmp, y, ALU.mult).then_inc(step_sem, 1)
                dve.wait_ge(step_sem, b.count(steps, 10))
                V.scalar_tensor_tensor(out=ln[:, 6, :], in0=ln[:, 5, :], scalar=-1.0, in1=rstd, op0=ALU.mult,
                                       op1=ALU.mult).then_inc(step_sem, 1)

            def x_stats(b):
                if isinstance(b.loop, int) and b.offset == 0:
                    dve.wait_ge(x_first, 16)
                else:
                    dve.wait_ge(x_loaded, b.count(16, 16))
                for t in range(T):
                    if t == T // 2 and isinstance(b.loop, int) and b.offset == 0:
                        dve.wait_ge(x_loaded, 16)
                    V.bn_stats(stat[:, t, :], x_in[:, t, :]).then_inc(x_stat, 1)
                variance(x_ln, x_stat, x_step, b, X_STEPS, DIN)

            def h0_lo(b, g):
                dve.wait_ge(h0_hi, b.count(GROUPS, g + 1))
                ts = slice(GT * g, GT * (g + 1))
                V.scalar_tensor_tensor(out=h0[:, ts, LO_AT:HL], in0=u[:, g % 2, :, :], scalar=H0_SCALE,
                                       in1=h0[:, ts, 0:DIN], op0=ALU.mult, op1=ALU.subtract).then_inc(h0_ready, 1)

            def incidence(b, q):
                dve.wait_ge(adj_loaded[q], b.count(16, 16))
                if q == 0:
                    wait_reuse(dve, e_done, b.count(T, -T))
                for ct in range(QT * q, QT * (q + 1)):
                    V.tensor_scalar(inc[:, b.slot, ct, :], adj_in[:, ct, :], 0.0, None,
                                    ALU.not_equal).then_inc(inc_ready, 1)

            def degree(b, ct):
                if ct == 0:
                    dve.wait_ge(w_loaded, b.count(16, 16))
                    dve.wait_ge(inc_ready, b.count(T, T))
                wait_reuse(dve, deg_done, b.count(T, ct))
                V.scalar_tensor_tensor(out=junk[:, :], in0=inc[:, b.slot, ct, :], scalar=1.0, in1=edge_w[:, :],
                                       op0=ALU.mult, op1=ALU.mult,
                                       accum_out=deg[:, ct:ct + 1]).then_inc(deg_done, 1)

            def node_inverse(b):
                dve.wait_ge(deg_done, b.count(T, T))
                V.tensor_scalar(dn_tmp[:, 0, :], deg[:, :], LEAST, None, ALU.max).then_inc(dn_step, 1)
                dve.wait_ge(dn_step, b.count(N_STEPS, 1))
                V.reciprocal(dn_tmp[:, 1, :], dn_tmp[:, 0, :]).then_inc(dn_step, 1)
                dve.wait_ge(dn_step, b.count(N_STEPS, 2))
                V.scalar_tensor_tensor(out=dn_tmp[:, 2, :], in0=deg[:, :], scalar=0.0, in1=dn_tmp[:, 1, :],
                                       op0=ALU.is_gt, op1=ALU.mult).then_inc(dn_step, 1)
                dve.wait_ge(dn_step, b.count(N_STEPS, 3))
                V.tensor_scalar(dn1[:, b.slot, :], dn_tmp[:, 2, :], wr[:, 4:5], None, ALU.mult).then_inc(dn_step, 1)
                V.tensor_scalar(dn2[:, b.slot, :], dn_tmp[:, 2, :], wr[:, 5:6], None, ALU.mult).then_inc(dn_step, 1)

            def b_lo(b, j):
                dve.wait_ge(pt_hi, b.count(4, j + 1))
                dt, half = j % 2, j // 2
                cols = slice(BANK * half, BANK * (half + 1))
                V.scalar_tensor_tensor(out=pt[:, dt, LO, cols], in0=wide[j][:, :], scalar=PT_SCALE,
                                       in1=pt[:, dt, HI, cols], op0=ALU.mult, op1=ALU.subtract).then_inc(pt_ready, 1)

            def phase_b(b, bx, bi=None):
                if bx is not None:
                    x_stats(bx)
                b_lo(b, 0)
                if bx is not None:
                    inverse_root(x_ln, x_step, bx, X_STEPS, 1.0)
                    if bi is not None:
                        incidence(bi, 0)
                        incidence(bi, 1)
                    h0_lo(bx, 0)
                b_lo(b, 1)
                if bx is not None:
                    h0_lo(bx, 1)
                    if bi is not None:
                        incidence(bi, 2)
                        incidence(bi, 3)
                    h0_lo(bx, 2)
                b_lo(b, 2)
                if bx is not None:
                    h0_lo(bx, 3)
                b_lo(b, 3)

            def phase_c(b):
                if isinstance(b.loop, int) and b.offset == 0:
                    dve.wait_ge(rows_loaded, 32)
                for t in range(T + 1):
                    if t < T:
                        dve.wait_ge(c_done, b.count(T, t + 1))
                        if t == 0:
                            dve.wait_ge(dn_step, b.count(N_STEPS, N_STEPS))
                            wait_reuse(dve, d_done, b.count(T, 0))
                        V.scalar_tensor_tensor(out=z[:, t, :], in0=wide[t % 4][:, :], scalar=dn1[:, b.slot, t:t + 1],
                                               in1=b1_row[:, :], op0=ALU.mult, op1=ALU.add).then_inc(c_drained, 1)
                    if t >= 1:
                        dve.wait_ge(z_relu, b.count(T, t))
                        V.bn_stats(stat[:, t - 1, :], z[:, t - 1, :]).then_inc(z_stat, 1)
                variance(z_ln, z_stat, z_step, b, Z_STEPS, DH)

            def z_lo(b, t):
                dve.wait_ge(zs_hi, b.count(T, t + 1))
                V.tensor_tensor(zs[:, t % ZRING, LO, :], z[:, t, :], zs[:, t % ZRING, HI, :],
                                ALU.subtract).then_inc(zs_ready, 1)

            def phase_d(b, bd=None):
                def add_bias(t):
                    dve.wait_ge(d_done, b.count(T, t + 1))
                    if t >= 2:
                        dve.wait_ge(xw_ready, b.count(T, t - 1))
                    V.scalar_tensor_tensor(out=xf[:, t % 2, :], in0=narrow[t % 4][:, 0:DOUT], scalar=XW_SCALE,
                                           in1=bw_row[:, :], op0=ALU.mult, op1=ALU.add).then_inc(xf_ready, 1)

                def xw_lo(t):
                    dve.wait_ge(xw_hi, b.count(T, t + 1))
                    V.tensor_tensor(xw[:, t, LO, :], xf[:, t % 2, :], xw[:, t, HI, :],
                                    ALU.subtract).then_inc(xw_ready, 1)

                for t in range(T):
                    add_bias(t)
                    if t >= 1:
                        xw_lo(t - 1)
                    if bd is not None and t in EARLY_DEGREES:
                        degree(bd, EARLY_DEGREES.index(t))
                xw_lo(T - 1)

            def phase_e(b, bd):
                for et in range(T):
                    dve.wait_ge(t2_hi, b.count(T, et + 1))
                    V.scalar_tensor_tensor(out=edge[:, et, LO, :], in0=narrow[et % 4][:, 0:DOUT],
                                           scalar=be[:, b.slot, et:et + 1], in1=edge[:, et, HI, :],
                                           op0=ALU.mult, op1=ALU.subtract).then_inc(t2_ready, 1)
                    ct = et + len(EARLY_DEGREES)
                    if bd is not None and ct < T:
                        degree(bd, ct)
                    if bd is not None and ct == T:
                        node_inverse(bd)

            def phase_f(b, bi, bz):
                if bz is not None:
                    inverse_root(z_ln, z_step, bz, Z_STEPS, ZN_SCALE)
                for ct in range(T):
                    if bi is not None and ct < QUARTERS:
                        incidence(bi, ct)
                    dve.wait_ge(f_done, b.count(T, ct + 1))
                    if ct == 0:
                        dve.wait_ge(res_ready, b.count(1, 1))
                    V.scalar_tensor_tensor(out=res[:, b.slot, ct, :], in0=narrow[ct % 4][:, 0:DOUT],
                                           scalar=dn2[:, b.slot, ct:ct + 1], in1=res[:, b.slot, ct, :],
                                           op0=ALU.mult, op1=ALU.add).then_inc(out_ready, 1)
                    if bz is not None and ct >= Z_BEHIND:
                        z_lo(bz, ct - Z_BEHIND)

            def bank_of_a(b, et):
                return first_banks[et] if isinstance(b.loop, int) and b.offset == 0 else narrow[et % 4]

            def edge_inverse(b, et):
                dve.wait_ge(a_done, b.count(T, et + 1))
                V.tensor_scalar(be_cnt[:, et:et + 1], bank_of_a(b, et)[:, ONE:ONE + 1], 1.0, None,
                                ALU.max).then_inc(be_step, 1)
                dve.wait_ge(be_step, b.count(2 * T, 2 * et + 1))
                V.reciprocal(be[:, b.slot, et:et + 1], be_cnt[:, et:et + 1]).then_inc(be_step, 1)

            def t1_lo_part(b, et):
                dve.wait_ge(t1_hi, b.count(T, et + 1))
                V.scalar_tensor_tensor(out=edge[:, et, LO, :], in0=bank_of_a(b, et)[:, 0:DIN],
                                       scalar=be[:, b.slot, et:et + 1], in1=edge[:, et, HI, :],
                                       op0=ALU.mult, op1=ALU.subtract).then_inc(t1_ready, 1)

            def phase_a(b, bz):
                for et in range(T):
                    edge_inverse(b, et)
                    if et < Z_BEHIND:
                        z_lo(bz, T - Z_BEHIND + et)
                    t1_lo_part(b, et)

            def largest(i, src):
                return V.tensor_reduce(wm[:, i:i + 1], src, mybir.AxisListType.XY, ALU.max,
                                       apply_absolute_value=True)

            b0 = Batch(0, 0)
            x_stats(b0)
            dve.wait_ge(weights_loaded, 48)
            for ht in range(HT_):
                last = V.tensor_copy(beta_cols[:, ht, :], gb[:, 1, ht:ht + 1].to_broadcast([P, P]))
            last.then_inc(beta_ready, 1)
            inverse_root(x_ln, x_step, b0, X_STEPS, 1.0)
            incidence(b0, 0)
            h0_lo(b0, 0)
            dve.wait_ge(bias_done, 1)
            largest(2, narrow[3][:, None, 0:DOUT])
            V.tensor_copy(bw_row[:, :], narrow[3][:, 0:DOUT]).then_inc(bias_read, 1)
            dve.wait_ge(gamma_w2, 1)
            largest(1, gf)
            for q in range(1, QUARTERS):
                h0_lo(b0, q)
                incidence(b0, q)
                if q == 1:
                    dve.wait_ge(w1_loaded, 16)
                    largest(0, w1f).then_inc(setup_step, 1)
            dve.wait_ge(setup_step, 1)
            V.scalar_tensor_tensor(out=wm[:, 1:2], in0=wm[:, 2:3], scalar=BIAS_ROOM, in1=wm[:, 1:2],
                                   op0=ALU.mult, op1=ALU.max).then_inc(max_here, 1)
            for et in range(T):
                edge_inverse(b0, et)
                degree(b0, et)
                t1_lo_part(b0, et)
                if et == T - 2:
                    dve.wait_ge(max_all, 1)
                    V.tensor_scalar(wall[:, :], wall[:, :], TINY, None, ALU.max).then_inc(setup_step, 1)
                    dve.wait_ge(setup_step, 2)
                    V.tensor_scalar(wp[:, :].bitcast(U32), wall[:, :].bitcast(U32), EXPONENT, None,
                                    ALU.bitwise_and).then_inc(setup_step, 1)
                    dve.wait_ge(setup_step, 3)
                    V.reciprocal(wr[:, 0:2], wp[:, :])
                    V.tensor_scalar(wr[:, 4:5], wp[:, 0:1], 1.0 / (H0_SCALE * PT_SCALE * W_SCALE), None, ALU.mult)
                    V.tensor_scalar(wr[:, 5:6], wp[:, 1:2], 1.0 / (ZN_SCALE * W_SCALE * XW_SCALE), None,
                                    ALU.mult).then_inc(setup_step, 1)
                    dve.wait_ge(setup_step, 4)
                    V.tensor_scalar(wr[:, 2:4], wr[:, 0:2], W_SCALE, None, ALU.mult).then_inc(setup_step, 1)
            V.tensor_scalar(bw_row[:, :], bw_row[:, :], wr[:, 1:2], ZN_SCALE * W_SCALE * XW_SCALE,
                            ALU.mult, ALU.mult).then_inc(setup_step, 1)
            node_inverse(b0)
            phase_b(b0, Batch(0, 1), Batch(0, 1))
            phase_c(b0)
            inverse_root(z_ln, z_step, b0, Z_STEPS, ZN_SCALE)
            for t in range(T):
                edge_inverse(Batch(0, 1), t)
                z_lo(b0, t)
                t1_lo_part(Batch(0, 1), t)
            with dve.Fori(0, N - 2, 2) as n:
                for k in range(2):
                    phase_d(Batch(n, k), Batch(n, k + 1))
                    phase_b(Batch(n, k + 1), Batch(n, k + 2))
                    phase_e(Batch(n, k), Batch(n, k + 1))
                    phase_c(Batch(n, k + 1))
                    phase_f(Batch(n, k), Batch(n, k + 2), Batch(n, k + 1))
                    phase_a(Batch(n, k + 2), Batch(n, k + 1))
            phase_d(Batch(0, N - 2), Batch(0, N - 1))
            phase_b(Batch(0, N - 1), None)
            phase_e(Batch(0, N - 2), Batch(0, N - 1))
            phase_c(Batch(0, N - 1))
            phase_f(Batch(0, N - 2), None, Batch(0, N - 1))
            for t in range(T - Z_BEHIND, T):
                z_lo(Batch(0, N - 1), t)
            phase_d(Batch(0, N - 1))
            phase_e(Batch(0, N - 1), None)
            phase_f(Batch(0, N - 1), None, None)
    return nc


def kernel(x, adj, L0_gnn_W1, L0_gnn_b1, L0_gnn_gamma, L0_gnn_beta, L0_gnn_W2, L0_gnn_b2):
    import numpy as np
    import concourse.bacc as bacc
    from concourse.bass_utils import run_bass_kernel_spmd as run

    arrays = {
        "x": np.ascontiguousarray(x),
        "adj": np.ascontiguousarray(adj),
        "w1t": np.ascontiguousarray(np.transpose(L0_gnn_W1)),
        "b1": np.ascontiguousarray(np.reshape(L0_gnn_b1, (1, -1))),
        "gamma": np.ascontiguousarray(np.transpose(np.reshape(L0_gnn_gamma, (-1, P)))),
        "beta": np.ascontiguousarray(np.transpose(np.reshape(L0_gnn_beta, (-1, P)))),
        "w2t": np.ascontiguousarray(np.transpose(L0_gnn_W2)),
        "b2": np.ascontiguousarray(np.reshape(L0_gnn_b2, (1, -1))),
    }
    nc = bacc.Bacc("TRN2", target_bir_lowering=False, num_devices=1)
    ins = [nc.dram_tensor(name, a.shape, mybir.dt.from_np(a.dtype), kind="ExternalInput").ap()
           for name, a in arrays.items()]
    out = nc.dram_tensor("out", arrays["x"].shape, F32, kind="ExternalOutput").ap()
    hypergraph_block(nc, *ins, out)
    return run(nc, [arrays], core_ids=[0]).results[0]["out"]
```
